# Optimizing a Trainium2 kernel written in Bass

```python
import numpy as np
import jax
import jax.numpy as jnp

def _softmax(x, axis=-1):
    return jax.nn.softmax(x, axis=axis)

def _gelu(x):
    return jax.nn.gelu(x, approximate=True)

def _silu(x):
    return jax.nn.silu(x)

def _sigmoid(x):
    return jax.nn.sigmoid(x)

def _layernorm(x, axis=-1, eps=1e-05):
    m = jnp.mean(x, axis=axis, keepdims=True)
    v = jnp.var(x, axis=axis, keepdims=True)
    return (x - m) / jnp.sqrt(v + eps)

def _scatter_add(tgt, idx, src, axis=0):
    return tgt.at[idx].add(src)

def _segment_sum(src, seg, n):
    return jax.ops.segment_sum(src, seg, n)
kernel_name = 'mk_adj_preln_d4_adj_r2_b9b0d0'

def setup_inputs(seed: int=0):
    np.random.seed(seed)
    _w = jnp.asarray

    def _rec_inputs():
        import jax
        import jax.numpy as jnp
        _gk = jax.random.key(seed)
        x = -0.0005207 + 1.001 * jax.random.normal(jax.random.fold_in(_gk, 1), (8, 1024, 128), jnp.float32)
        _w = (1.0 + jnp.arange(1024, dtype=jnp.float32)) ** (-0.5)
        _w = _w / _w.mean()
        _pij = jnp.clip(0.0078125 * _w[:, None] * _w[None, :], 0.0, 1.0)
        _a = jax.random.uniform(jax.random.fold_in(_gk, 2), (8, 1024, 1024)) < _pij
        adj = _a.astype(jnp.int32)
        return (x, adj)
    x, adj = _rec_inputs()

    def _L0_gnn_setup():
        import jax, jax.numpy as jnp
        import numpy as np
        B, N, DIN, H, D = (16, 512, 128, 4, 32)
        NEG = -9000000000000000.0
        key = jax.random.key(seed)
        k1, k2, k3, k4 = jax.random.split(key, 4)
        x = jax.random.normal(k1, (B, N, DIN), jnp.float32)
        adj = jax.random.randint(k2, (B, N, N), 0, 2, jnp.int32)
        W = jax.random.normal(k3, (DIN, H * D), jnp.float32) * np.float32(1.0 / np.sqrt(DIN))
        b = jnp.zeros((H * D,), jnp.float32)
        a = jax.random.normal(k4, (2 * D, 1), jnp.float32) * np.float32(0.1)
        return {'x': x, 'adj': adj, 'W': W, 'b': b, 'a': a}
    _L0_gnn_all = _L0_gnn_setup()
    _L0_gnn_in = {k: v for k, v in _L0_gnn_all.items() if k in ('W', 'b', 'a')}
    del _L0_gnn_all

    def _L1_gnn_setup():
        import jax, jax.numpy as jnp
        import numpy as np
        BN_EPS = 0.001
        NEG_INF = -1e+30

        def _masked_row_softmax(adjT):
            mask = adjT != 0
            logits = jnp.where(mask, adjT, NEG_INF)
            p = jax.nn.softmax(logits, axis=-1)
            return jnp.where(mask, p, 0.0)

        def _batch_norm(x, gamma, beta):
            mean = jnp.mean(x, axis=(0, 1), keepdims=True)
            var = jnp.var(x, axis=(0, 1), keepdims=True)
            return (x - mean) * jax.lax.rsqrt(var + BN_EPS) * gamma + beta
        key = jax.random.key(seed)
        ks = jax.random.split(key, 4)
        B, N, F = (1, 4096, 128)
        C0, C1 = (128, 128)
        features = jax.random.normal(ks[0], (B, N, F), dtype=jnp.float32)
        adj = jax.random.randint(ks[1], (B, N, N), 0, 2, dtype=jnp.int32)
        kernel_1 = jax.random.normal(ks[2], (F, C0), dtype=jnp.float32) * (1.0 / np.sqrt(F))
        kernel_2 = jax.random.normal(ks[3], (C0, C1), dtype=jnp.float32) * (1.0 / np.sqrt(C0))
        return {'features': features, 'adj': adj, 'kernel_1': kernel_1, 'bias_1': jnp.zeros((C0,), jnp.float32), 'gamma_1': jnp.ones((C0,), jnp.float32), 'beta_1': jnp.zeros((C0,), jnp.float32), 'kernel_2': kernel_2, 'bias_2': jnp.zeros((C1,), jnp.float32), 'gamma_2': jnp.ones((C1,), jnp.float32), 'beta_2': jnp.zeros((C1,), jnp.float32)}
    _L1_gnn_all = _L1_gnn_setup()
    _L1_gnn_in = {k: v for k, v in _L1_gnn_all.items() if k in ('kernel_1', 'bias_1', 'gamma_1', 'beta_1', 'kernel_2', 'bias_2', 'gamma_2', 'beta_2')}
    del _L1_gnn_all

    def _L2_gnn_setup():
        import jax, jax.numpy as jnp
        import numpy as np
        ALPHA = 0.2
        NEG = -9000000000000000.0
        key = jax.random.key(seed)
        ks = jax.random.split(key, 6)
        B, N, F, H, D = (16, 256, 128, 8, 32)
        x = jax.random.normal(ks[0], (B, N, F), dtype=jnp.float32)
        adj = jax.random.randint(ks[1], (B, N, N), 0, 2, dtype=jnp.int32)
        W1 = jax.random.normal(ks[2], (H, F, D), dtype=jnp.float32) * (1.414 * (6.0 / (F + D)) ** 0.5)
        a1 = jax.random.normal(ks[3], (H, 2 * D), dtype=jnp.float32) * 0.2
        W2 = jax.random.normal(ks[4], (H * D, F), dtype=jnp.float32) * (1.414 * (6.0 / (H * D + F)) ** 0.5)
        a2 = jax.random.normal(ks[5], (2 * F,), dtype=jnp.float32) * 0.2
        return {'x': x, 'adj': adj, 'W1': W1, 'a1': a1, 'W2': W2, 'a2': a2}
    _L2_gnn_all = _L2_gnn_setup()
    _L2_gnn_in = {k: v for k, v in _L2_gnn_all.items() if k in ('W1', 'a1', 'W2', 'a2')}
    del _L2_gnn_all

    def _L3_gnn_setup():
        import jax, jax.numpy as jnp
        import numpy as np
        ALPHA = 0.2
        NEG_INF = -1000000000.0
        key = jax.random.key(seed)
        k1, k2, k3, k4 = jax.random.split(key, 4)
        B, N, F_in, F_out = (4, 2048, 128, 128)
        h = jax.random.normal(k1, (B, N, F_in), dtype=jnp.float32)
        adj = jax.random.randint(k2, (B, N, N), 0, 2, dtype=jnp.int32)
        limW = np.sqrt(6.0 / (F_in + F_out))
        W = jax.random.uniform(k3, (F_in, F_out), jnp.float32, -limW, limW)
        lima = np.sqrt(6.0 / (2 * F_out + 1))
        a = jax.random.uniform(k4, (2 * F_out,), jnp.float32, -lima, lima)
        return {'h': h, 'adj': adj, 'W': W, 'a': a}
    _L3_gnn_all = _L3_gnn_setup()
    _L3_gnn_in = {k: v for k, v in _L3_gnn_all.items() if k in ('W', 'a')}
    del _L3_gnn_all
    return {'x': x, 'adj': adj, 'L0_gnn_W': _L0_gnn_in['W'], 'L0_gnn_b': _L0_gnn_in['b'], 'L0_gnn_a': _L0_gnn_in['a'], 'L1_gnn_kernel_1': _L1_gnn_in['kernel_1'], 'L1_gnn_bias_1': _L1_gnn_in['bias_1'], 'L1_gnn_gamma_1': _L1_gnn_in['gamma_1'], 'L1_gnn_beta_1': _L1_gnn_in['beta_1'], 'L1_gnn_kernel_2': _L1_gnn_in['kernel_2'], 'L1_gnn_bias_2': _L1_gnn_in['bias_2'], 'L1_gnn_gamma_2': _L1_gnn_in['gamma_2'], 'L1_gnn_beta_2': _L1_gnn_in['beta_2'], 'L2_gnn_W1': _L2_gnn_in['W1'], 'L2_gnn_a1': _L2_gnn_in['a1'], 'L2_gnn_W2': _L2_gnn_in['W2'], 'L2_gnn_a2': _L2_gnn_in['a2'], 'L3_gnn_W': _L3_gnn_in['W'], 'L3_gnn_a': _L3_gnn_in['a']}

def reference(x, adj, L0_gnn_W, L0_gnn_b, L0_gnn_a, L1_gnn_kernel_1, L1_gnn_bias_1, L1_gnn_gamma_1, L1_gnn_beta_1, L1_gnn_kernel_2, L1_gnn_bias_2, L1_gnn_gamma_2, L1_gnn_beta_2, L2_gnn_W1, L2_gnn_a1, L2_gnn_W2, L2_gnn_a2, L3_gnn_W, L3_gnn_a):
    import jax
    import jax.numpy as jnp

    def _L0_gnn_ref(x, adj, W, b, a):
        import jax, jax.numpy as jnp
        import numpy as np
        B, N, DIN, H, D = (16, 512, 128, 4, 32)
        NEG = -9000000000000000.0
        Bb, Nn, _ = x.shape
        h = (x @ W + b).reshape(Bb, Nn, H, D)
        a_i, a_j = (a[:D, 0], a[D:, 0])
        e_i = jnp.einsum('bnhd,d->bnh', h, a_i)
        e_j = jnp.einsum('bnhd,d->bnh', h, a_j)
        e = e_i[:, :, None, :] + e_j[:, None, :, :]
        e = jnp.where(e > 0, e, 0.2 * e)
        e = jnp.where(adj[..., None] > 0, e, NEG)
        attn = jax.nn.softmax(e, axis=2)
        out = jnp.einsum('bijh,bjhd->bihd', attn, h)
        return out.reshape(Bb, Nn, H * D)

    def _L1_gnn_ref(features, adj, kernel_1, bias_1, gamma_1, beta_1, kernel_2, bias_2, gamma_2, beta_2):
        import jax, jax.numpy as jnp
        import numpy as np
        BN_EPS = 0.001
        NEG_INF = -1e+30

        def _masked_row_softmax(adjT):
            mask = adjT != 0
            logits = jnp.where(mask, adjT, NEG_INF)
            p = jax.nn.softmax(logits, axis=-1)
            return jnp.where(mask, p, 0.0)

        def _batch_norm(x, gamma, beta):
            mean = jnp.mean(x, axis=(0, 1), keepdims=True)
            var = jnp.var(x, axis=(0, 1), keepdims=True)
            return (x - mean) * jax.lax.rsqrt(var + BN_EPS) * gamma + beta
        adjT = jnp.transpose(adj.astype(jnp.float32), (0, 2, 1))
        w = _masked_row_softmax(adjT)
        region = jnp.matmul(w, features)
        region = jnp.matmul(region, kernel_1) + bias_1
        region = _batch_norm(region, gamma_1, beta_1)
        people = jnp.matmul(jnp.transpose(w, (0, 2, 1)), region)
        people = jnp.matmul(people, kernel_2) + bias_2
        people = _batch_norm(people, gamma_2, beta_2)
        return people

    def _L2_gnn_ref(x, adj, W1, a1, W2, a2):
        import jax, jax.numpy as jnp
        import numpy as np
        ALPHA = 0.2
        NEG = -9000000000000000.0
        mask = adj > 0
        h = jnp.einsum('bnf,hfd->bhnd', x, W1)
        D = h.shape[-1]
        f1 = jnp.einsum('bhnd,hd->bhn', h, a1[:, :D])
        f2 = jnp.einsum('bhnd,hd->bhn', h, a1[:, D:])
        e = jax.nn.leaky_relu(f1[..., :, None] + f2[..., None, :], ALPHA)
        e = jnp.where(mask[:, None, :, :], e, NEG)
        att = jax.nn.softmax(e, axis=-1)
        hp = jnp.einsum('bhij,bhjd->bhid', att, h)
        hp = jax.nn.elu(hp)
        B, H, N, Dh = hp.shape
        xc = hp.transpose(0, 2, 1, 3).reshape(B, N, H * Dh)
        h2 = jnp.einsum('bnk,kc->bnc', xc, W2)
        C = h2.shape[-1]
        g1 = jnp.einsum('bnc,c->bn', h2, a2[:C])
        g2 = jnp.einsum('bnc,c->bn', h2, a2[C:])
        e2 = jax.nn.leaky_relu(g1[:, :, None] + g2[:, None, :], ALPHA)
        e2 = jnp.where(mask, e2, NEG)
        att2 = jax.nn.softmax(e2, axis=-1)
        hp2 = jnp.einsum('bij,bjc->bic', att2, h2)
        return jax.nn.elu(hp2) + x

    def _L3_gnn_ref(h, adj, W, a):
        import jax, jax.numpy as jnp
        import numpy as np
        ALPHA = 0.2
        NEG_INF = -1000000000.0
        F_out = W.shape[1]
        Wh = jnp.einsum('bnf,fo->bno', h, W)
        a_i, a_j = (a[:F_out], a[F_out:])
        si = Wh @ a_i
        sj = Wh @ a_j
        e = si[:, :, None] + sj[:, None, :]
        e = jnp.where(e > 0, e, ALPHA * e)
        e = jnp.where(adj > 0, e, NEG_INF)
        attention = jax.nn.softmax(e, axis=-1)
        h_prime = jnp.einsum('bij,bjo->bio', attention, Wh)
        return jax.nn.elu(h_prime)
    h = jnp.maximum(_layernorm(x, axis=-1), 0.0)
    x = x + _L0_gnn_ref(h, adj, L0_gnn_W, L0_gnn_b, L0_gnn_a)
    h = jnp.maximum(_layernorm(x, axis=-1), 0.0)
    x = x + _L1_gnn_ref(h, adj, L1_gnn_kernel_1, L1_gnn_bias_1, L1_gnn_gamma_1, L1_gnn_beta_1, L1_gnn_kernel_2, L1_gnn_bias_2, L1_gnn_gamma_2, L1_gnn_beta_2)
    h = jnp.maximum(_layernorm(x, axis=-1), 0.0)
    x = x + _L2_gnn_ref(h, adj, L2_gnn_W1, L2_gnn_a1, L2_gnn_W2, L2_gnn_a2)
    h = jnp.maximum(_layernorm(x, axis=-1), 0.0)
    x = x + _L3_gnn_ref(h, adj, L3_gnn_W, L3_gnn_a)
    return x

_drawn_inputs = setup_inputs


def setup_inputs(seed=0):
    import zlib

    import numpy as np

    out = dict(_drawn_inputs(seed))
    spreads = {'L0_gnn_b': (0.0, 0.1),
     'L1_gnn_bias_1': (0.0, 0.8),
     'L1_gnn_gamma_1': (1.0, 0.2),
     'L1_gnn_beta_1': (0.0, 0.1),
     'L1_gnn_bias_2': (0.0, 0.8),
     'L1_gnn_gamma_2': (1.0, 0.2),
     'L1_gnn_beta_2': (0.0, 0.1)}
    factors = {'L3_gnn_a': 3.032}
    for name, (base, spread) in spreads.items():
        noise = np.random.default_rng([zlib.crc32(name.encode()), seed]).standard_normal(out[name].shape)
        drawn = base * np.exp(spread * noise) if base else spread * noise
        out[name] = jnp.asarray(drawn.astype(out[name].dtype))
    for name, factor in factors.items():
        out[name] = (out[name] * factor).astype(out[name].dtype)
    return out
```

```python
from contextlib import ExitStack

import concourse.bass as bass
from concourse import mybir

ALU = mybir.AluOpType
ACT = mybir.ActivationFunctionType
AX = mybir.AxisListType
F32 = mybir.dt.float32
BF16 = mybir.dt.bfloat16
I32 = mybir.dt.int32
U8 = mybir.dt.uint8

P = 128
BANK = 512
LN_EPS = 1e-5
BN_EPS = 1e-3
SLOPE = 0.2
LIFT = 60.0
BIG = float(2 ** 60)
NT = 8
NG = 4


def gnn_stack(nc, x, adj, L0_W, L0_b, L0_a, k1, bias1, gamma1, beta1, k2, bias2, gamma2, beta2,
              W1, a1, W2, a2, L3_W, L3_a, out):
    B, N, F = x.shape
    NTL = N // P
    HALVES = N // BANK
    EDGES = [0, 3, 6, 8]
    assert F == P and NTL == 8 and HALVES == 2

    HB = B // 2

    class Layer:
        def __init__(self, name, H, D, K, act_tiles):
            self.name, self.H, self.D, self.K = name, H, D, K
            self.W = D + 1
            self.HD, self.NC = H * D, H * D + 2 * H
            self.wide = H == 1
            self.act_tiles = act_tiles

        def turn(self, b):
            return {LA: b + 0, LB: b + B, LC: 2 * b, LD: 2 * b + 1}[self]

        def head(self, b, h):
            return b * self.H + h + (B * LA.H if self is LB else 0)

    TA = (0, 1, 3, 4, 6, 7)
    LA = Layer("l0", 4, L0_W.shape[1] // 4, 1, TA)
    LB = Layer("l2a", W1.shape[0], W1.shape[2], 1, TA)
    LC = Layer("l2b", 1, W2.shape[1], W2.shape[0] // P, ())
    LD = Layer("l3", 1, L3_W.shape[1], 1, ())
    LAYERS = [LA, LB, LC, LD]
    HM, HWM = LB.H, LB.H * LB.W
    GC = 3 * P
    NGR = len(EDGES) - 1
    NS = 3

    ORDER_A = (("T0", 0), ("PC", -1), ("T1", 0), ("K0", 0), ("X0", 1), ("T2", 0), ("K1", 0), ("X1", 1), ("T3", 0),
               ("K2", 0), ("nA", 1), ("K3", 0), ("nF", 0), ("PA", 0), ("Pz", -1), ("XT", 1), ("nB", 1), ("PB", 0), ("nC", 1),
               ("Xz", 1), ("PG", 0), ("nD", 1), ("M", 1))
    ORDER_B = (("Bl", 1), ("Ba", 1), ("Bg", 0))
    ORDER_C = (("T0", 0), ("CA", -1), ("CB", -1), ("T1", 0), ("K0", 0), ("T2", 0), ("K1", 0), ("CC", -1), ("T3", 0),
               ("K2", 0), ("CD", -1), ("T4", 0), ("K3", 0), ("C0", -1), ("T5", 0), ("K4", 0), ("C1", -1), ("C2", -1),
               ("T6", 0), ("K5", 0), ("CF", -1), ("DA", -1), ("T7", 0), ("K6", 0), ("DB", -1), ("K7", 0), ("nF", 0),
               ("DC", -1), ("nA", 1), ("DD", -1), ("D0", -1), ("nB", 1), ("D1", -1), ("nC", 1), ("D2", -1),
               ("ML", 1), ("nD", 1), ("DF", -1), ("M", 1))

    def walk(eng, order, piece):
        def iteration(b):
            for name, off in order:
                if 0 <= b + off < B:
                    piece(name, b + off, (b + off) % 2)

        iteration(-1)
        iteration(0)
        with eng.Fori(0, HB - 1) as i:
            for name, off in order:
                piece(name, i * 2 + (1 + off), 1 ^ (off & 1))
            for name, off in order:
                piece(name, i * 2 + (2 + off), off & 1)
        iteration(B - 1)
        iteration(B)

    x_t = x.rearrange("b (t p) f -> b p t f", p=P)
    out_t = out.rearrange("b (t p) f -> b p t f", p=P)
    x1_dram = nc.dram_tensor("x1_scratch", (B, P, NTL, F), F32, kind="Internal").ap()
    y1_dram = nc.dram_tensor("y1_scratch", (B, P, N), F32, kind="Internal").ap()
    y2_dram = nc.dram_tensor("y2_scratch", (B, P, N), F32, kind="Internal").ap()
    mask_dram = nc.dram_tensor("mask_scratch", (B, P, NTL, N), BF16, kind="Internal").ap()
    f1_dram = {L: nc.dram_tensor(f"f1_{L.name}", (B, L.H, N), F32, kind="Internal").ap() for L in LAYERS}

    with ExitStack() as ctx:
        def sb(name, shape, dt=F32):
            return ctx.enter_context(nc.sbuf_tensor(name, shape, dt))

        def sem(name):
            return ctx.enter_context(nc.semaphore(name))

        maskbuf = sb("maskbuf", [P, 2, NTL, N], BF16)
        tu = sb("tu", [P, NTL, N], BF16)
        T = sb("T", [P, NT, N], BF16)
        G = sb("G", [P, NG, N], BF16)
        F1N = sb("F1N", [P, 2, N])
        F1W = sb("F1W", [P, 1, N])
        XpN = sb("XpN", [P, NTL * 6 * HWM], BF16)
        XpW = sb("XpW", [P, NTL * 6 * LD.W], BF16)
        scratch = sb("scratch", [P, NTL * HWM])
        hfN = sb("hfN", [P, NTL * HWM])
        hfW = sb("hfW", [P, NTL * LD.W])
        oN = sb("oN", [P, NTL * LB.HD])
        oW = sb("oW", [P, NTL * LD.HD])
        xcN, xsN, xnN, xcW, xnW = (sb(n, [P, NTL, F]) for n in ("xcN", "xsN", "xnN", "xcW", "xnW"))
        uN = sb("uN", [P, NTL * LB.W])
        uW = sb("uW", [P, NTL * LD.W])
        twf = tu[:, :, :].rearrange("p s n -> p (s n)")
        TW = twf[:, 0:NTL * GC].rearrange("p (s n) -> p s n", n=GC)
        UW = twf[:, NTL * GC:2 * NTL * GC].rearrange("p (s n) -> p s n", n=GC)
        xrN = T[:, :, :].rearrange("p s n -> p (s n)").bitcast(F32)[:, 0:8 * HWM].rearrange("p (c s n) -> p c s n", c=2, s=2)
        xrW = twf.bitcast(F32)[:, 0:8 * LD.W].rearrange("p (c s n) -> p c s n", c=2, s=2)
        adj_nat = (maskbuf[:, 1], tu)
        stage = XpN[:, 6 * NTL * LA.H * LA.W:].bitcast(I32)[:, 0:NS * N].rearrange("p (s n) -> p s n", s=NS)
        parts = (XpN[:, 0:3 * N].rearrange("p (t k f) -> p t k f", k=3, f=F),
                 XpW[:, 0:3 * N].rearrange("p (t k f) -> p t k f", k=3, f=F))
        identF = sb("identF", [P, P])
        identB = sb("identB", [P, P], BF16)
        ones = sb("ones", [P, P])
        cmean = sb("cmean", [P, P])
        wcat = {L: sb(f"wcat_{L.name}", [P, L.K, L.NC]) for L in LAYERS}
        bcat = sb("bcat", [P, LA.NC])
        k1s, k2s = sb("k1s", [P, P]), sb("k2s", [P, P])
        cols = sb("cols", [P, 8])
        mhalf, lneps = sb("mhalf", [P, NTL]), sb("lneps", [P, NTL])
        pad = sb("pad", [P, 1])
        outdeg, indeg, rin, empty = (sb(n, [P, NTL]) for n in ("outdeg", "indeg", "rin", "empty"))
        empty_all = sb("empty_all", [P, B, NTL])
        rin_all = sb("rin_all", [P, B, NTL])
        bst = [sb(f"bst{n}", [P, B * HALVES, 6]) for n in range(2)]
        bmv, bsc = sb("bmv", [P, 2, 2]), sb("bsc", [P, 2, 4])
        ps = ctx.enter_context(nc.psum_tensor("ps", [P, 8, BANK], F32))

        class Stream:
            def __init__(self, c, bank, H, **named):
                self.c, self.bank = c, bank
                self.t = dict(named)
                self.t.update({n: sb(f"{n}{c}", [P, H, NTL]) for n in ("g2", "nf2", "nbf2", "cpos", "crow")})
                self.t.update({n: sb(f"{n}{c}", [P, NTL]) for n in ("nm", "vpe", "rstd", "nmr")})
                self.t.update(ff=sb(f"ff{c}", [P, 2 * H, NTL]), bb=sb(f"bb{c}", [P, 2, H, NTL]),
                              st=sb(f"st{c}", [P, NTL, 6]), mv=sb(f"mv{c}", [P, NTL, 2]), mx=sb(f"mx{c}", [P, 1]),
                              diag=sb(f"diag{c}", [P, 2 * H]), m2=sb(f"m2{c}", [P, 2 * H]),
                              den=sb(f"den{c}", [P, 2, NTL]), empty=sb(f"empty{c}", [P, NTL]),
                              meanb=sb(f"meanb{c}", [P, LB.H * LB.W if c == "N" else LD.W]))
                self.s = {n: sem(f"{n}_{c}") for n in (
                    "proj_ps", "f", "hf", "frow_ps", "frow", "frow_out", "f1_0", "mean_ps", "mean", "mx", "diag",
                    "m2_ps", "m2", "g2", "c0", "c1", "expo", "xf", "xhi", "xr", "xmid", "xlo", "fin", "emin",
                    "eexp", "elu", "t", "t_used", "cmb", "free", "hT_ps", "hinT",
                    "stats", "moments", "nmr1", "pow", "rstd", "xn")}
                self.s.update({n: sem(n) for n in (("f1_1", "g", "ms_ps", "ms") if c == "N" else ("u",))})

        SN = Stream("N", 0, LB.H, hf=hfN, o=oN, u=uN, Xp=XpN, xr=xrN, xn=xnN)
        SW = Stream("W", 4, 1, hf=hfW, o=oW, u=uW, Xp=XpW, xr=xrW, xn=xnW)
        for L in LAYERS:
            L.S = SW if L.wide else SN

        atmp = uW[:, 0:512]
        abc = {LA: scratch[:, 1024:1088], LB: scratch[:, 0:512], LC: scratch[:, 512:768], LD: scratch[:, 768:1024]}
        q = {n: sem(n) for n in (
            "w_in", "sp_waits", "cst", "wprod", "wred", "adj_in0", "adj_in1", "adj_in2", "adj_cvt", "mT_ps", "mT",
            "mask_out", "mask_in", "deg0", "deg", "x_in", "x1", "x1_out",
            "hi", "r1", "mid", "lo", "reg_ps", "reg",
            "regT_ps", "regT", "y1_ps", "y1", "y1s", "y1_out", "bag0", "bpow0", "bs0", "bt0", "bag1", "bpow1", "bs1",
            "bt1", "y1_in", "z", "G_ps", "Gf", "y2_ps", "y2", "y2s", "y2_out",
            "y2_in", "x1_in", "yn", "ynT_ps", "x2", "emp", "empW", "l2a", "xsum", "x3", "out_x", "out")}

        block = ctx.enter_context(nc.Block())

        def hinT_of(L):
            if L.wide:
                return XpW[:, 0:2 * L.K * N].bitcast(F32)
            return scratch[:, L.H * L.W * NTL:][:, 0:N] if L is LA else scratch[:, 0:N]

        def frow_of(L):
            return uW[:, 0:N] if L.wide else hfN[:, L.H * L.W * NTL:][:, 0:N] if L is LA else scratch[:, N:2 * N]

        def ms_view(L):
            return scratch[:, 0:NTL * L.H * L.W].rearrange("p (t h w) -> p t h w", h=L.H, w=L.W)

        def hf_view(L):
            return L.S.t["hf"][:, 0:NTL * L.H * L.W].rearrange("p (t h w) -> p t h w", h=L.H, w=L.W)

        def o_view(L):
            return L.S.t["o"][:, 0:NTL * L.HD].rearrange("p (t h d) -> p t h d", h=L.H, d=L.D)

        def xp_view(L):
            return L.S.t["Xp"][:, 0:NTL * 6 * L.H * L.W].rearrange("p (t k h c w) -> p t k h c w", k=3, h=L.H, c=2,
                                                                 w=L.W)

        def xt_view(which, L, t):
            return L.S.t["xr"][:, which, t % 2, 0:2 * L.H * L.W].rearrange("p (h c w) -> p h c w", c=2, w=L.W)

        def mask_of(L, par):
            return maskbuf[:, 0] if L is LA else maskbuf[:, par]

        def x_of(par):
            return (xcN, xsN)[par]

        def norm_turn(L, b):
            return b + 0 if L is LA or L is None else b + B

        def ones_before(L, t):
            return sum(1 for a in L.act_tiles if a < t)

        def wide_of(name):
            return LC if name[0] == "C" else LD

        @block.sync
        def _(sp):
            for dst, src in (
                (wcat[LA][:, 0, 0:LA.HD], L0_W), (k1s[:, :], k1), (k2s[:, :], k2),
                (wcat[LB][:, 0, 0:LB.HD].rearrange("p (h d) -> p h d", h=LB.H), W1.rearrange("h f d -> f h d")),
                (wcat[LC][:, :, 0:LC.HD], W2.rearrange("(k p) n -> p k n", p=P)),
                (wcat[LD][:, 0, 0:LD.HD], L3_W),
                (bcat[:, 0:LA.HD], L0_b.rearrange("(a n) -> a n", a=1).to_broadcast((P, LA.HD))),
                (abc[LA], L0_a.rearrange("n a -> a n").to_broadcast((P, 64))),
                (abc[LB], a1.rearrange("(a h) n -> a (h n)", a=1).to_broadcast((P, 512))),
                (abc[LC], a2.rearrange("(a n) -> a n", a=1).to_broadcast((P, 256))),
                (abc[LD], L3_a.rearrange("(a n) -> a n", a=1).to_broadcast((P, 256))),
                *((cols[:, n:n + 1], v.rearrange("(p a) -> p a", a=1))
                  for n, v in enumerate((bias1, gamma1, beta1, bias2, gamma2, beta2))),
            ):
                sp.dma_start(dst, src).then_inc(q["w_in"], 16)

            def wait(s, value):
                sp.wait_ge(s, value)
                sp.sem_inc(q["sp_waits"], 1)

            def store_f_rows(L, b):
                s = L.S.s
                wait(s["frow"], L.turn(b) + 1)
                sp.dma_start(f1_dram[L][b], frow_of(L)[0:L.H, :]).then_inc(s["frow_out"], 16)
                wait(s["frow_out"], L.turn(b) * 16 + 16)

            def load_f1(L, b, h):
                s = L.S.s
                if L.wide:
                    wait(s["t"], L.turn(b) * (NGR * NTL) + NGR * NTL)
                    sp.dma_start(F1W[:, 0, :], f1_dram[L][b].to_broadcast((P, N))).then_inc(s["f1_0"], 16)
                else:
                    wait(s["t"], L.head(b, h) * NTL + NTL)
                    sp.dma_start(F1N[:, h % 2, :], f1_dram[L][b, h:h + 1, :].to_broadcast((P, N)))\
                        .then_inc(s[f"f1_{h % 2}"], 16)

            def piece_a(name, b, par):
                if name in ("X0", "X1"):
                    for t in range(*((0, 4) if name == "X0" else (4, NTL))):
                        wait(q["adj_cvt"], b * NTL + (t + 1))
                        sp.dma_start(stage[:, (t % NS), :], adj[b, t * P:(t + 1) * P, :])\
                            .then_inc(q[f"adj_in{t % NS}"], 16)
                elif name == "nA":
                    sp.dma_start(x_of(par)[:, :, :], x_t[b]).then_inc(q["x_in"], 16)
                elif name == "nC":
                    store_f_rows(LA, b)
                    load_f1(LA, b, 0)
                elif name[0] == "T" and int(name[1]) + 1 < LA.H:
                    load_f1(LA, b, int(name[1]) + 1)
                elif name == "XT":
                    wait(q["mT"], b * NTL + NTL)
                    sp.dma_start(mask_dram[b], maskbuf[:, 0]).then_inc(q["mask_out"], 16)
                elif name == "PA":
                    wait(q["x1"], b + 1)
                    sp.dma_start(x1_dram[b], xcW[:, :, :]).then_inc(q["x1_out"], 16)
                elif name == "PC":
                    wait(q["y1"], 2 * b + 2)
                    sp.dma_start(y1_dram[b], hfW[:, 0:N]).then_inc(q["y1_out"], 16)

            def piece_b(name, b, par):
                if name == "Bl":
                    wait(q["y2s"], b * 2 + 1)
                    sp.dma_start(maskbuf[:, par], mask_dram[b]).then_inc(q["mask_in"], 16)
                    wait(q["z"], b + 1)
                    sp.dma_start(hfN[:, 0:N], y1_dram[b]).then_inc(q["y1_in"], 16)
                    wait(q["y1_in"], b * 16 + 16)
                    wait(q["mask_in"], b * 16 + 16)
                elif name == "Bg":
                    wait(q["y2"], 2 * b + 2)
                    sp.dma_start(y2_dram[b], hfW[:, 0:N]).then_inc(q["y2_out"], 16)

            def piece_c(name, b, par):
                if name == "nA":
                    wait(q["xsum"], b + 1)
                    sp.dma_start(xnN[:, :, :].rearrange("p t f -> p (t f)"), y2_dram[b]).then_inc(q["y2_in"], 16)
                    sp.dma_start(xcN[:, :, :], x1_dram[b]).then_inc(q["x1_in"], 16)
                elif name == "nC":
                    store_f_rows(LB, b)
                    load_f1(LB, b, 0)
                elif name[0] == "T" and int(name[1]) + 1 < LB.H:
                    load_f1(LB, b, int(name[1]) + 1)
                elif name == "ML":
                    wait(q["x3"], b + 1)
                    sp.dma_start(maskbuf[:, par], mask_dram[b]).then_inc(q["mask_in"], 16)
                elif name in ("CC", "DC"):
                    store_f_rows(wide_of(name), b)
                    load_f1(wide_of(name), b, 0)
                elif name == "DF":
                    wait(q["x3"], b + 3)
                    sp.dma_start(out_t[b], xcW[:, :, :]).then_inc(q["out"], 16)

            walk(sp, ORDER_A, piece_a)
            wait(q["y1_out"], B * 16 + 16)
            wait(q["x1_out"], B * 16 + 16)
            wait(q["mask_out"], B * 16 + 16)
            walk(sp, ORDER_B, piece_b)
            wait(q["y2_out"], B * 16 + 16)
            walk(sp, ORDER_C, piece_c)
            sp.wait_ge(q["out"], B * 16 + 16)

        def pool_rstd(pool, S, turn):
            s, t = S.s, S.t
            pool.wait_ge(s["moments"], turn * NTL + NTL)
            nc.gpsimd.tensor_tensor(t["vpe"][:, :], t["mv"][:, :, 1], lneps[:, :], ALU.add).then_inc(s["nmr1"], 1)
            nc.gpsimd.tensor_scalar(t["nm"][:, :], t["mv"][:, :, 0], -1.0, None, ALU.mult).then_inc(s["nmr1"], 1)
            pool.wait_ge(s["nmr1"], turn * 2 + 2)
            nc.gpsimd.tensor_tensor(t["rstd"][:, :], t["vpe"][:, :], mhalf[:, :], ALU.pow).then_inc(s["pow"], 1)
            pool.wait_ge(s["pow"], turn + 1)
            nc.gpsimd.tensor_tensor(t["nmr"][:, :], t["nm"][:, :], t["rstd"][:, :], ALU.mult).then_inc(s["rstd"], 1)

        def pool_parts(pool, b, L):
            s = L.S.s
            for t in range(NTL + 1):
                if t < NTL:
                    if t >= 2:
                        pool.wait_ge(s["xlo"], L.turn(b) * NTL + (t - 1))
                    pool.wait_ge(s["xhi"], L.turn(b) * NTL + (t + 1))
                    nc.gpsimd.tensor_tensor(xt_view(1, L, t), xt_view(0, L, t), xp_view(L)[:, t, 0], ALU.subtract)\
                        .then_inc(s["xr"], 1)
                if t >= 1:
                    pool.wait_ge(s["xmid"], L.turn(b) * NTL + t)
                    nc.gpsimd.tensor_tensor(xp_view(L)[:, t - 1, 2], xt_view(1, L, t - 1), xp_view(L)[:, t - 1, 1],
                                            ALU.subtract).then_inc(s["xlo"], 1)

        def pool_complement(pool, b, par, L, g):
            s = L.S.s
            n = (EDGES[g + 1] - EDGES[g]) * P
            for jt in range(NTL):
                at = L.turn(b) * (NGR * NTL) + (g * NTL + jt + 1)
                pool.wait_ge(s["t"], at + NGR * NTL)
                pool.wait_ge(s["t_used"], at)
                nc.gpsimd.tensor_tensor(UW[:, jt, 0:n], mask_of(L, par)[:, jt, EDGES[g] * P:EDGES[g + 1] * P],
                                        TW[:, jt, 0:n], ALU.subtract).then_inc(s["u"], 1)

        @block.gpsimd
        def _(pool):
            pool.memset(identF[:, :], 0.0).then_inc(q["cst"], 1)
            pool.memset(ones[:, :], 1.0).then_inc(q["cst"], 1)
            pool.memset(cmean[:, :], 1.0 / N).then_inc(q["cst"], 1)
            pool.memset(mhalf[:, :], -0.5).then_inc(q["cst"], 1)
            pool.memset(lneps[:, :], LN_EPS).then_inc(q["cst"], 1)
            pool.memset(cols[:, 6:7], LIFT).then_inc(q["cst"], 1)
            pool.wait_ge(q["cst"], 6)
            pool.affine_select(out=identF[:, :], in_=identF[:, :], compare_op=ALU.not_equal, fill=1.0, base=0,
                               pattern=[[-1, P]], channel_multiplier=1).then_inc(q["cst"], 1)
            pool.wait_ge(q["cst"], 7)
            pool.tensor_copy(identB[:, :], identF[:, :]).then_inc(q["cst"], 1)

            def piece_a(name, b, par):
                if name == "nA":
                    pool_rstd(pool, SN, norm_turn(LA, b))
                elif name == "nD":
                    pool_parts(pool, b, LA)
                elif name == "PA":
                    pool_rstd(pool, SW, norm_turn(None, b))

            def piece_c(name, b, par):
                if name == "nA":
                    pool_rstd(pool, SN, norm_turn(LB, b))
                elif name == "nD":
                    pool_parts(pool, b, LB)
                elif name == "DA":
                    pool_rstd(pool, SW, norm_turn(LD, b))
                elif name in ("CD", "DD"):
                    pool_parts(pool, b, wide_of(name))
                elif name in ("C0", "C1", "C2", "D0", "D1", "D2"):
                    pool_complement(pool, b, par, wide_of(name), int(name[1]))

            walk(pool, ORDER_A, piece_a)
            for n in range(2):
                pool.wait_ge(q[f"bag{n}"], 2)
                pool.tensor_tensor(bsc[:, n, 1:2], bsc[:, n, 0:1], mhalf[:, 0:1], ALU.pow)\
                    .then_inc(q[f"bpow{n}"], 1)
            walk(pool, ORDER_C, piece_c)

        def act_b(act, b, L):
            s, bank = L.S.s, L.S.bank
            for k in range(L.K):
                for h in range(HALVES):
                    n = k * HALVES + h
                    act.wait_ge(s["hT_ps"], hT_before(L, b) + (n + 1))
                    nc.scalar.activation(hinT_of(L)[:, n * BANK:(n + 1) * BANK], ps[:, hT_bank(L, n), :],
                                         ACT.Copy if L is LC else ACT.Relu).then_inc(s["hinT"], 1)

        def hT_before(L, b):
            return HALVES * L.turn(b) if not L.wide else b * (HALVES * (LC.K + LD.K)) + (HALVES * LC.K if L is LD else 0)

        def hT_bank(L, n):
            return 4 + n if L.wide else 2 + n

        def act_c(act, b, L):
            s, t, H2 = L.S.s, L.S.t, 2 * L.H
            fb = 4 if L.wide else 2
            act.wait_ge(s["frow_ps"], HALVES * L.turn(b) + HALVES)
            nc.scalar.activation(frow_of(L)[0:H2, :].rearrange("p (a n) -> p a n", a=2), ps[0:H2, fb:fb + 2, :],
                                 ACT.Copy).then_inc(s["frow"], 1)
            act.wait_ge(s["mean_ps"], L.turn(b) + 1)
            nc.scalar.activation(t["meanb"][:, 0:L.H * L.W], ps[:, L.S.bank + (2 if L.wide else 0), 0:L.H * L.W],
                                 ACT.Copy).then_inc(s["mean"], 1)
            act.wait_ge(s["g2"], L.turn(b) + 1)
            nc.scalar.activation(t["bb"][:, 0, 0:L.H, :], t["g2"][:, 0:L.H, :], ACT.Exp, bias=cols[:, 6:7])\
                .then_inc(s["expo"], 1)
            nc.scalar.activation(t["bb"][:, 1, 0:L.H, :], t["g2"][:, 0:L.H, :], ACT.Exp, scale=SLOPE)\
                .then_inc(s["expo"], 1)
            act.wait_ge(s["c1"], L.turn(b) + 1)
            nc.scalar.activation(t["crow"][:, 0:L.H, :], t["cpos"][:, 0:L.H, :], ACT.Exp, scale=SLOPE - 1.0,
                                 bias=cols[:, 6:7]).then_inc(s["expo"], 1)

        def act_d(act, b, L):
            s = L.S.s
            for t in range(NTL + 1):
                if t < NTL:
                    act.wait_ge(s["xf"], L.turn(b) * NTL + (t + 1))
                    nc.scalar.activation(xp_view(L)[:, t, 0], xt_view(0, L, t), ACT.Copy).then_inc(s["xhi"], 1)
                if t >= 1:
                    act.wait_ge(s["xr"], L.turn(b) * NTL + t)
                    nc.scalar.activation(xp_view(L)[:, t - 1, 1], xt_view(1, L, t - 1), ACT.Copy)\
                        .then_inc(s["xmid"], 1)

        def act_sums(act, b, L):
            s = L.S.s
            act.wait_ge(s["frow_out"], L.turn(b) * 16 + 16)
            for it in range(NTL):
                act.wait_ge(s["ms_ps"], L.turn(b) * NTL + (it + 1))
                nc.scalar.activation(ms_view(L)[:, it], ps[:, it % 2, 0:L.H * L.W].rearrange(
                    "p (h w) -> p h w", h=L.H), ACT.Copy).then_inc(s["ms"], 1)

        def act_signs(act, b, L, h):
            s, na = L.S.s, len(L.act_tiles)
            act.wait_ge(s[f"f1_{h % 2}"], f1_count(L, b, h))
            for n, jt in enumerate(L.act_tiles):
                c = (h % 2) * na + n
                back = (c - NG) % (2 * na)
                act.wait_ge(s["t"], L.head(b, h - h % 2) * NTL + (
                    2 * NTL + (back // na) * NTL + L.act_tiles[back % na] + 1 - (2 * NTL if c < NG else 0)))
                nc.scalar.activation(G[:, c % NG, :], F1N[:, h % 2, :], ACT.Relu, scale=-BIG,
                                     bias=L.S.t["nbf2"][:, h, jt:jt + 1]).then_inc(s["g"], 1)

        def f1_count(L, b, h):
            return (b * (L.H // 2) + (h // 2 + 1 + (B * LA.H // 2 if L is LB else 0))) * 16

        def elu_turn(L, b):
            return b + 0 if L is LB else L.turn(b)

        def act_elu(act, b, L):
            act.wait_ge(L.S.s["emin"], elu_turn(L, b) + 1)
            hf = L.S.t["hf"]
            nc.scalar.activation(hf[:, 0:NTL * L.HD], hf[:, 0:NTL * L.HD], ACT.Exp).then_inc(L.S.s["eexp"], 1)

        @block.scalar
        def _(act):
            act.wait_ge(q["cst"], 8)
            act.sem_inc(q["adj_cvt"], NS)
            act.sem_inc(q["z"], 1)

            def n_piece(name, b, par, L):
                if name == "nB":
                    act_b(act, b, L)
                elif name == "nC":
                    act_c(act, b, L)
                elif name == "nD":
                    act_d(act, b, L)
                elif name == "M":
                    act_sums(act, b, L)
                elif name[0] == "T":
                    act_signs(act, b, L, int(name[1]))

            def piece_a(name, b, par):
                n_piece(name, b, par, LA)
                if name in ("X0", "X1"):
                    for t in range(*((0, 4) if name == "X0" else (4, NTL))):
                        k = t % NS
                        per = len(range(k, NTL, NS))
                        act.wait_ge(q[f"adj_in{k}"], b * (16 * per) + (16 * (t // NS) + 16))
                        nc.scalar.activation(adj_nat[par][:, t, :], stage[:, k, :], ACT.Copy,
                                             accum_out=outdeg[:, t:t + 1]).then_inc(q["adj_cvt"], 1)
                elif name == "XT":
                    act.wait_ge(q["mask_out"], b * 16 + 16)
                    for t in range(NTL):
                        act.wait_ge(q["mT_ps"], b * NTL + (t + 1))
                        nc.scalar.activation(maskbuf[:, 0, t, :], ps[:, 4 + t % 4, :].bitcast(BF16), ACT.Copy,
                                             accum_out=indeg[:, t:t + 1]).then_inc(q["mT"], 1)
                elif name == "PB":
                    act.wait_ge(SW.s["xn"], norm_turn(None, b) * NTL + NTL)
                    nc.scalar.activation(parts[1][:, :, 0, :], xnW[:, :, :], ACT.Relu).then_inc(q["hi"], 1)
                    act.wait_ge(q["r1"], b + 1)
                    nc.scalar.activation(parts[1][:, :, 1, :], oW[:, :].rearrange("p (t f) -> p t f", f=F), ACT.Copy)\
                        .then_inc(q["mid"], 1)
                elif name == "PG":
                    for t in range(NTL):
                        act.wait_ge(q["reg_ps"], b * NTL + (t + 1))
                        nc.scalar.activation(xnW[:, t, :], ps[:, 4 + t % 4, 0:P], ACT.Copy,
                                             scale=rin_all[:, b, t:t + 1]).then_inc(q["reg"], 1)
                elif name == "PC":
                    for h in range(HALVES):
                        act.wait_ge(q["regT_ps"], 2 * b + (h + 1))
                        nc.scalar.activation(oW[:, h * BANK:(h + 1) * BANK], ps[:, 4 + h, :], ACT.Copy)\
                            .then_inc(q["regT"], 1)
                    for h in range(HALVES):
                        act.wait_ge(q["y1_ps"], 2 * b + (h + 1))
                        if h == 0:
                            act.wait_ge(q["y1_out"], b * 16 + 16)
                        nc.scalar.activation(hfW[:, h * BANK:(h + 1) * BANK], ps[:, 6 + h, :], ACT.Identity,
                                             bias=cols[:, 0:1]).then_inc(q["y1"], 1)

            def piece_b(name, b, par):
                if name == "Ba":
                    act.wait_ge(q["y1_in"], b * 16 + 16)
                    nc.scalar.activation(scratch[:, 0:N], hfN[:, 0:N], ACT.Identity, scale=bsc[:, 0, 2:3],
                                         bias=bsc[:, 0, 3:4]).then_inc(q["z"], 1)
                    for t in range(NTL):
                        if t % 4 == 0:
                            act.wait_ge(q["G_ps"], 2 * b + (t // 4 + 1))
                        nc.scalar.activation(xnN[:, t, :], ps[:, 4 + t // 4, (t % 4) * P:(t % 4 + 1) * P], ACT.Copy,
                                             scale=rin_all[:, b, t:t + 1]).then_inc(q["Gf"], 1)
                    act.wait_ge(q["Gf"], b * NTL + NTL)
                    nc.scalar.activation(parts[par][:, :, 0, :], xnN[:, :, :], ACT.Copy).then_inc(q["hi"], 1)
                    act.wait_ge(q["r1"], b + (B + 1))
                    nc.scalar.activation(parts[par][:, :, 1, :], oN[:, 0:N].rearrange("p (t f) -> p t f", f=F),
                                         ACT.Copy).then_inc(q["mid"], 1)
                elif name == "Bg":
                    act.wait_ge(q["y2_out"], b * 16 + 16)
                    act.wait_ge(q["y2s"], 2 * b + 4)
                    for h in range(HALVES):
                        act.wait_ge(q["y2_ps"], 2 * b + (h + 1))
                        nc.scalar.activation(hfW[:, h * BANK:(h + 1) * BANK], ps[:, 2 * par + h, :], ACT.Identity,
                                             bias=cols[:, 3:4]).then_inc(q["y2"], 1)

            def piece_c(name, b, par):
                if name == "nA":
                    act.wait_ge(q["y2_in"], b * 16 + 16)
                    xf = xnN[:, :, :].rearrange("p t f -> p (t f)")
                    nc.scalar.activation(xf, xf, ACT.Identity, scale=bsc[:, 1, 2:3], bias=bsc[:, 1, 3:4])\
                        .then_inc(q["yn"], 1)
                n_piece(name, b, par, LB)
                if name == "nF":
                    act_elu(act, b, LB)
                elif name in ("CB", "DB"):
                    act_b(act, b, wide_of(name))
                elif name in ("CC", "DC"):
                    act_c(act, b, wide_of(name))
                elif name in ("CD", "DD"):
                    act_d(act, b, wide_of(name))
                elif name in ("CF", "DF"):
                    act_elu(act, b, wide_of(name))

            walk(act, ORDER_A, piece_a)
            act.wait_ge(q["bt0"], 1)
            walk(act, ORDER_B, piece_b)
            act.wait_ge(q["bt1"], 1)
            walk(act, ORDER_C, piece_c)

        def dve_norm(dve, S, turn, xc):
            s, st, mv, xn, rstd, nmr = S.s, *(S.t[n] for n in ("st", "mv", "xn", "rstd", "nmr"))
            for t in range(NTL):
                nc.vector.bn_stats(st[:, t, :], xc[:, t, :]).then_inc(s["stats"], 1)
            dve.wait_ge(s["stats"], turn * NTL + NTL)
            nc.vector.memset(pad[:, :], 0.0)
            for t in range(NTL):
                nc.vector.bn_aggr(mv[:, t, :], st[:, t, :]).then_inc(s["moments"], 1)
            dve.wait_ge(s["rstd"], turn + 1)
            for t in range(NTL):
                nc.vector.tensor_scalar(xn[:, t, :], xc[:, t, :], rstd[:, t:t + 1], nmr[:, t:t + 1],
                                        ALU.mult, ALU.add).then_inc(s["xn"], 1)

        def dve_b(dve, b, L):
            s, H, H2, bank, ff = L.S.s, L.H, 2 * L.H, L.S.bank, L.S.t["ff"]
            hv = hf_view(L)
            nc.vector.memset(hv[:, :, :, L.D:L.W], 1.0).then_inc(s["hf"], 1)
            for t in range(NTL):
                dve.wait_ge(s["proj_ps"], L.turn(b) * NTL + (t + 1))
                pj = ps[:, proj_bank(L, t), :]
                src = pj[:, 0:L.HD].rearrange("p (h d) -> p h d", h=H)
                if L is LA:
                    nc.vector.tensor_tensor(ff[:, 0:H2, t], pj[:, L.HD:L.NC], bcat[:, L.HD:L.NC], ALU.add)\
                        .then_inc(s["f"], 1)
                    nc.vector.tensor_tensor(hv[:, t, :, 0:L.D], src,
                                            bcat[:, 0:L.HD].rearrange("p (h d) -> p h d", h=H), ALU.add)\
                        .then_inc(s["hf"], 1)
                else:
                    nc.vector.tensor_copy(ff[:, 0:H2, t], pj[:, L.HD:L.NC]).then_inc(s["f"], 1)
                    nc.vector.tensor_copy(hv[:, t, :, 0:L.D], src).then_inc(s["hf"], 1)

        def proj_bank(L, t):
            return (6 if L.wide else 0) + t % 2

        def dve_c(dve, b, L):
            s, H, H2 = L.S.s, L.H, 2 * L.H
            mx, diag, m2, g2, cpos, nf2, nbf2, ff = (L.S.t[n] for n in (
                "mx", "diag", "m2", "g2", "cpos", "nf2", "nbf2", "ff"))
            dve.wait_ge(s["frow"], L.turn(b) + 1)
            nc.vector.tensor_reduce(mx[0:H2, :], frow_of(L)[0:H2, :], axis=AX.X, op=ALU.max).then_inc(s["mx"], 1)
            dve.wait_ge(s["mx"], L.turn(b) + 1)
            nc.vector.tensor_scalar(diag[0:H2, 0:H2], identF[0:H2, 0:H2], mx[0:H2, :], None, ALU.mult)\
                .then_inc(s["diag"], 1)
            dve.wait_ge(s["m2_ps"], L.turn(b) + 1)
            nc.vector.tensor_copy(m2[:, 0:H], ps[:, 7 if L.wide else 1, H:H2]).then_inc(s["m2"], 1)
            dve.wait_ge(s["m2"], L.turn(b) + 1)
            m2v = m2[:, 0:H].unsqueeze(2).to_broadcast((P, H, NTL))
            nc.vector.tensor_tensor(g2[:, 0:H, :], ff[:, H:H2, :], m2v, ALU.subtract).then_inc(s["g2"], 1)
            nc.vector.tensor_tensor(cpos[:, 0:H, :], ff[:, 0:H, :], m2v, ALU.add).then_inc(s["c0"], 1)
            nc.vector.tensor_scalar(nf2[:, 0:H, :], ff[:, H:H2, :], -1.0, None, ALU.mult).then_inc(s["c0"], 1)
            nc.vector.tensor_scalar(nbf2[:, 0:H, :], ff[:, H:H2, :], -BIG, None, ALU.mult).then_inc(s["c0"], 1)
            dve.wait_ge(s["c0"], 3 * L.turn(b) + 3)
            nc.vector.tensor_scalar(cpos[:, 0:H, :], cpos[:, 0:H, :], 0.0, None, ALU.max).then_inc(s["c1"], 1)

        def dve_d(dve, b, L):
            s, H, bb, hv = L.S.s, L.H, L.S.t["bb"], hf_view(L)
            dve.wait_ge(s["expo"], 3 * L.turn(b) + 3)
            dve.wait_ge(s["hf"], L.turn(b) * (NTL + 1) + (NTL + 1))
            for t in range(NTL):
                if t >= 2:
                    dve.wait_ge(s["xr"], L.turn(b) * NTL + (t - 1))
                nc.vector.tensor_tensor(
                    xt_view(0, L, t), hv[:, t].unsqueeze(2).to_broadcast((P, H, 2, L.W)),
                    bb[:, :, 0:H, t].rearrange("p c h -> p h c").unsqueeze(3).to_broadcast((P, H, 2, L.W)),
                    ALU.mult).then_inc(s["xf"], 1)

        def dve_divide(dve, L, h, src, step):
            s, den, empty = L.S.s, L.S.t["den"], L.S.t["empty"]
            nc.vector.tensor_tensor(den[:, 0, :], src[:, :, L.D], empty[:, :], ALU.add).then_inc(s["cmb"], 1)
            dve.wait_ge(s["cmb"], step + 1)
            nc.vector.reciprocal(den[:, 1, :], den[:, 0, :]).then_inc(s["cmb"], 1)
            dve.wait_ge(s["cmb"], step + 2)
            nc.vector.tensor_tensor(o_view(L)[:, :, h, :], src[:, :, 0:L.D],
                                    den[:, 1, :].unsqueeze(2).to_broadcast((P, NTL, L.D)), ALU.mult)\
                .then_inc(s["cmb"], 1)

        def dve_combine(dve, b, L, h):
            s, u, k = L.S.s, L.S.t["u"], 1 - h % 2
            head = L.head(b, h)
            step = head * 6 + 1
            dve.wait_ge(s["t_used"], head * NTL + (NT + NTL))
            dve.wait_ge(s["ms"], L.turn(b) * NTL + NTL)
            acc = ps[:, 2 * k:2 * k + 2, 0:4 * 2 * L.W].rearrange("p a (t c w) -> p a t c w", c=2, w=L.W)
            uv = u[:, 0:NTL * L.W].rearrange("p (a t w) -> p a t w", a=2, w=L.W)
            ut = u[:, 0:NTL * L.W].rearrange("p (t w) -> p t w", w=L.W)
            dve.wait_ge(s["cmb"], step)
            for a in range(2):
                nc.vector.tensor_tensor(uv[:, a], ms_view(L)[:, 4 * a:4 * a + 4, h, :], acc[:, a, :, 1, :],
                                        ALU.subtract).then_inc(s["cmb"], 1)
            dve.wait_ge(s["cmb"], step + 2)
            nc.vector.tensor_tensor(ut, ut, L.S.t["crow"][:, h, :].unsqueeze(2).to_broadcast((P, NTL, L.W)), ALU.mult)\
                .then_inc(s["cmb"], 1)
            dve.wait_ge(s["cmb"], step + 3)
            nc.vector.tensor_tensor(uv, uv, acc[:, :, :, 0, :], ALU.add).then_inc(s["free"], 1)
            dve.wait_ge(s["free"], head + 3)
            dve_divide(dve, L, h, ut, step + 3)

        def dve_thresholds(dve, b, par, L, h):
            s, na, k = L.S.s, len(L.act_tiles), h % 2
            head, mask = L.head(b, h), mask_of(L, par)
            dve.wait_ge(s[f"f1_{k}"], f1_count(L, b, h))
            for jt in range(NTL):
                dve.wait_ge(s["t_used"], head * NTL + (jt + 1))
                if jt in L.act_tiles:
                    n = ones_before(L, jt)
                    dve.wait_ge(s["g"], head * na + (n + 1))
                    nc.vector.tensor_tensor(T[:, jt % NT, :], mask[:, jt, :], G[:, (k * na + n) % NG, :], ALU.is_gt)\
                        .then_inc(s["t"], 1)
                else:
                    nc.vector.scalar_tensor_tensor(
                        out=T[:, jt % NT, :], in0=F1N[:, k, :], scalar=L.S.t["nf2"][:, h, jt:jt + 1],
                        in1=mask[:, jt, :], op0=ALU.is_gt, op1=ALU.mult).then_inc(s["t"], 1)

        def dve_group(dve, b, par, L, g):
            s = L.S.s
            n = (EDGES[g + 1] - EDGES[g]) * P
            mask = mask_of(L, par)
            at = slice(EDGES[g] * P, EDGES[g + 1] * P)
            if g == 0:
                dve.wait_ge(s["f1_0"], L.turn(b) * 16 + 16)
                dve.wait_ge(s["c0"], 3 * L.turn(b) + 3)
                dve.wait_ge(s["xlo"], L.turn(b) * NTL + NTL)
            for jt in range(NTL):
                dve.wait_ge(s["t_used"], L.turn(b) * (NGR * NTL) + (g * NTL + jt + 1))
                nc.vector.scalar_tensor_tensor(
                    out=TW[:, jt, 0:n], in0=F1W[:, 0, at], scalar=L.S.t["nf2"][:, 0, jt:jt + 1],
                    in1=mask[:, jt, at], op0=ALU.is_gt, op1=ALU.mult).then_inc(s["t"], 1)

        def dve_combine_group(dve, b, L, g):
            s = L.S.s
            lo, hi = EDGES[g], EDGES[g + 1]
            n, bank = hi - lo, 4 + 2 * (g % 2)
            ut = uW[:, :].rearrange("p (t w) -> p t w", w=L.W)[:, lo:hi]
            tv, uv = (ps[:, bank + c, 0:n * L.W].rearrange("p (t w) -> p t w", w=L.W) for c in range(2))
            dve.wait_ge(s["t_used"], L.turn(b) * (NGR * NTL) + ((g + 1) * NTL + NTL))
            nc.vector.tensor_tensor(ut, uv, L.S.t["crow"][:, 0, lo:hi].unsqueeze(2).to_broadcast((P, n, L.W)),
                                    ALU.mult).then_inc(s["cmb"], 1)
            dve.wait_ge(s["cmb"], L.turn(b) * 6 + (g + 1))
            nc.vector.tensor_tensor(ut, ut, tv, ALU.add).then_inc(s["free"], 1)

        def dve_mean(dve, b, L):
            s, empty = L.S.s, L.S.t["empty"]
            dve.wait_ge(s["cmb"], L.turn(b) * 6 + 6 if L.wide else L.head(b, 0) * 6 + (6 * L.H + 1))
            dve.wait_ge(s["mean"], L.turn(b) + 1)
            mvw = L.S.t["meanb"][:, 0:L.H * L.W].rearrange("p (h w) -> p h w", w=L.W)[:, :, 0:L.D]
            for t in range(NTL):
                nc.vector.scalar_tensor_tensor(out=o_view(L)[:, t], in0=mvw, scalar=empty[:, t:t + 1],
                                               in1=o_view(L)[:, t], op0=ALU.mult, op1=ALU.add).then_inc(s["fin"], 1)
            dve.wait_ge(s["fin"], L.turn(b) * NTL + NTL)

        def dve_elu(dve, b, L):
            s, n, o, hf = L.S.s, NTL * L.HD, L.S.t["o"], L.S.t["hf"]
            nc.vector.tensor_scalar(hf[:, 0:n], o[:, 0:n], 0.0, None, ALU.min).then_inc(s["emin"], 1)
            dve.wait_ge(s["eexp"], elu_turn(L, b) + 1)
            nc.vector.scalar_tensor_tensor(out=o[:, 0:n], in0=o[:, 0:n], scalar=0.0, in1=hf[:, 0:n],
                                           op0=ALU.max, op1=ALU.add).then_inc(s["elu"], 1)
            dve.wait_ge(s["elu"], elu_turn(L, b) + 1)

        @block.vector
        def _(dve):
            for s, n in ((SN.s["t"], 2 * NTL), (SN.s["t_used"], NT), (SN.s["free"], 2), (SN.s["cmb"], 1),
                         (SW.s["t"], NGR * NTL), (SW.s["t_used"], NTL), (SW.s["free"], 2),
                         (q["mask_out"], 16), (q["y1_out"], 16), (q["y2_out"], 16), (q["x1_out"], 16), (q["y2s"], 4),
                         (q["xsum"], 1), (q["x3"], 2), (q["out"], 16), (q["y1s"], 2)):
                dve.sem_inc(s, n)
            wr = [0, 0]
            dve.wait_ge(q["w_in"], 17 * 16)

            def fold(dst, w, vec, H, D):
                av = atmp[:, 0:H * D].rearrange("p (h d) -> p h d", h=H)
                nc.vector.tensor_tensor(av, w, vec, ALU.mult).then_inc(q["wprod"], 1)
                wr[0] += 1
                dve.wait_ge(q["wprod"], wr[0])
                nc.vector.tensor_reduce(dst, av, axis=AX.X, op=ALU.add).then_inc(q["wred"], 1)
                wr[1] += 1
                dve.wait_ge(q["wred"], wr[1])

            for L in LAYERS:
                if L is LB:
                    av = abc[L].rearrange("p (h c d) -> p h c d", c=2, d=L.D)
                    vec = [av[:, :, c, :] for c in range(2)]
                else:
                    av = abc[L].rearrange("p (a c d) -> p a c d", a=1, c=2)
                    vec = [av[:, :, c, :].to_broadcast((P, L.H, L.D)) for c in range(2)]
                for c in range(2):
                    at = slice(L.HD + c * L.H, L.HD + (c + 1) * L.H)
                    for kk in range(L.K):
                        fold(wcat[L][:, kk, at], wcat[L][:, kk, 0:L.HD].rearrange("p (h d) -> p h d", h=L.H),
                             vec[c], L.H, L.D)
                    if L is LA:
                        fold(bcat[:, at], bcat[:, 0:L.HD].rearrange("p (h d) -> p h d", h=L.H), vec[c], L.H, L.D)
            dve.wait_ge(q["cst"], 8)

            def batchnorm(n):
                dve.wait_ge(q[f"y{n + 1}s"], B * HALVES + (2, 4)[n])
                nc.vector.bn_aggr(bmv[:, n, :], bst[n][:, :, :].rearrange("p a s -> p (a s)")).then_inc(q[f"bag{n}"], 1)
                dve.wait_ge(q[f"bag{n}"], 1)
                nc.vector.tensor_scalar(bsc[:, n, 0:1], bmv[:, n, 1:2], BN_EPS, None, ALU.add).then_inc(q[f"bag{n}"], 1)
                dve.wait_ge(q[f"bpow{n}"], 1)
                nc.vector.tensor_tensor(bsc[:, n, 2:3], bsc[:, n, 1:2], cols[:, 3 * n + 1:3 * n + 2], ALU.mult)\
                    .then_inc(q[f"bs{n}"], 1)
                dve.wait_ge(q[f"bs{n}"], 1)
                nc.vector.tensor_tensor(bsc[:, n, 1:2], bsc[:, n, 2:3], bmv[:, n, 0:1], ALU.mult)\
                    .then_inc(q[f"bs{n}"], 1)
                dve.wait_ge(q[f"bs{n}"], 2)
                nc.vector.tensor_tensor(bsc[:, n, 3:4], cols[:, 3 * n + 2:3 * n + 3], bsc[:, n, 1:2], ALU.subtract)\
                    .then_inc(q[f"bt{n}"], 1)

            def n_piece(name, b, par, L):
                if name == "nB":
                    dve_b(dve, b, L)
                elif name == "nC":
                    dve_c(dve, b, L)
                elif name == "nD":
                    dve_d(dve, b, L)
                elif name[0] == "T":
                    dve_thresholds(dve, b, par, L, int(name[1]))
                elif name[0] == "K":
                    dve_combine(dve, b, L, int(name[1]))

            flat = "p (t f) -> p t f"

            def piece_a(name, b, par):
                n_piece(name, b, par, LA)
                if name == "nA":
                    dve.wait_ge(q["x_in"], b * 16 + 16)
                    dve_norm(dve, SN, norm_turn(LA, b), x_of(par))
                elif name == "nC":
                    dve.wait_ge(q["mT"], b * NTL + NTL)
                    nc.vector.tensor_scalar(SN.t["empty"][:, :], outdeg[:, :], 0.0, None, ALU.is_equal)\
                        .then_inc(q["deg0"], 1)
                    nc.vector.tensor_scalar(rin[:, :], indeg[:, :], 1.0, None, ALU.max).then_inc(q["deg0"], 1)
                    dve.wait_ge(q["deg0"], 2 * b + 2)
                    nc.vector.tensor_copy(empty_all[:, b, :], SN.t["empty"][:, :]).then_inc(q["deg"], 1)
                    nc.vector.reciprocal(rin_all[:, b, :], rin[:, :]).then_inc(q["deg"], 1)
                elif name == "nF":
                    dve_mean(dve, b, LA)
                    dve.wait_ge(q["x1_out"], b * 16 + 16)
                    nc.vector.tensor_tensor(xcW[:, :, :], x_of(par)[:, :, :], oN[:, 0:N].rearrange(flat, f=F), ALU.add)\
                        .then_inc(q["x1"], 1)
                elif name == "PA":
                    dve.wait_ge(q["x1"], b + 1)
                    dve_norm(dve, SW, norm_turn(None, b), xcW)
                elif name == "PB":
                    r1 = oW[:, :].rearrange(flat, f=F)
                    dve.wait_ge(q["hi"], b + 1)
                    nc.vector.scalar_tensor_tensor(out=r1, in0=xnW[:, :, :], scalar=0.0, in1=parts[1][:, :, 0, :],
                                                   op0=ALU.max, op1=ALU.subtract).then_inc(q["r1"], 1)
                    dve.wait_ge(q["mid"], b + 1)
                    nc.vector.tensor_tensor(parts[1][:, :, 2, :], r1, parts[1][:, :, 1, :], ALU.subtract)\
                        .then_inc(q["lo"], 1)
                elif name == "PC":
                    for h in range(HALVES):
                        dve.wait_ge(q["y1"], 2 * b + (h + 1))
                        nc.vector.bn_stats(bst[0][:, b * HALVES + h, :], hfW[:, h * BANK:(h + 1) * BANK])\
                            .then_inc(q["y1s"], 1)

            def piece_b(name, b, par):
                if name == "Ba":
                    r1 = oN[:, 0:N].rearrange(flat, f=F)
                    dve.wait_ge(q["lo"], b + B)
                    dve.wait_ge(q["hi"], b + (B + 1))
                    nc.vector.tensor_tensor(r1, xnN[:, :, :], parts[par][:, :, 0, :], ALU.subtract)\
                        .then_inc(q["r1"], 1)
                    dve.wait_ge(q["mid"], b + (B + 1))
                    nc.vector.tensor_tensor(parts[par][:, :, 2, :], r1, parts[par][:, :, 1, :], ALU.subtract)\
                        .then_inc(q["lo"], 1)
                elif name == "Bg":
                    for h in range(HALVES):
                        dve.wait_ge(q["y2"], 2 * b + (h + 1))
                        nc.vector.bn_stats(bst[1][:, b * HALVES + h, :], hfW[:, h * BANK:(h + 1) * BANK])\
                            .then_inc(q["y2s"], 1)

            def piece_c(name, b, par):
                if name == "nA":
                    nc.vector.tensor_copy(SN.t["empty"][:, :], empty_all[:, b, :]).then_inc(q["emp"], 1)
                    dve.wait_ge(q["x1_in"], b * 16 + 16)
                    dve.wait_ge(q["ynT_ps"], 2 * b + 2)
                    for h in range(HALVES):
                        xv = xcN[:, 4 * h:4 * h + 4, :]
                        nc.vector.tensor_tensor(xv, xv, ps[:, h, :].rearrange(flat, f=F), ALU.add)\
                            .then_inc(q["x2"], 1)
                    dve.wait_ge(q["x2"], 2 * b + 2)
                    dve_norm(dve, SN, norm_turn(LB, b), xcN)
                n_piece(name, b, par, LB)
                if name == "T0":
                    dve.wait_ge(q["emp"], b + 1)
                elif name == "nF":
                    dve_mean(dve, b, LB)
                    dve_elu(dve, b, LB)
                    nc.vector.tensor_scalar(oN[:, :], oN[:, :], -1.0, None, ALU.add).then_inc(q["l2a"], 1)
                    nc.vector.scalar_tensor_tensor(out=xsN[:, :, :], in0=xnN[:, :, :], scalar=0.0, in1=xcN[:, :, :],
                                                   op0=ALU.max, op1=ALU.add).then_inc(q["xsum"], 1)
                elif name in ("CB", "DB"):
                    dve_b(dve, b, wide_of(name))
                elif name in ("CC", "DC"):
                    dve_c(dve, b, wide_of(name))
                elif name in ("CD", "DD"):
                    dve_d(dve, b, wide_of(name))
                elif name == "CA":
                    nc.vector.tensor_copy(SW.t["empty"][:, :], empty_all[:, b, :]).then_inc(q["empW"], 1)
                elif name == "DA":
                    dve_norm(dve, SW, norm_turn(LD, b), xcW)
                elif name in ("C0", "C1", "C2", "D0", "D1", "D2"):
                    L, g = wide_of(name), int(name[1])
                    dve_group(dve, b, par, L, g)
                    if g:
                        dve_combine_group(dve, b, L, g - 1)
                if name in ("CF", "DF"):
                    L = wide_of(name)
                    dve.wait_ge(q["empW"], b + 1)
                    dve_combine_group(dve, b, L, NGR - 1)
                    dve.wait_ge(SW.s["free"], L.turn(b) * NGR + (NGR + 2))
                    dve_divide(dve, L, 0, uW[:, :].rearrange("p (t w) -> p t w", w=L.W), L.turn(b) * 6 + NGR)
                    dve_mean(dve, b, L)
                    dve_elu(dve, b, L)
                    ov = oW[:, :].rearrange(flat, f=F)
                    if L is LC:
                        dve.wait_ge(q["out"], b * 16 + 16)
                        nc.vector.scalar_tensor_tensor(out=xcW[:, :, :], in0=ov, scalar=-1.0, in1=xsN[:, :, :],
                                                       op0=ALU.add, op1=ALU.add).then_inc(q["out_x"], 1)
                        dve.wait_ge(q["out_x"], b + 1)
                    else:
                        nc.vector.scalar_tensor_tensor(out=xcW[:, :, :], in0=ov, scalar=-1.0, in1=xcW[:, :, :],
                                                       op0=ALU.add, op1=ALU.add).then_inc(q["x3"], 1)

            walk(dve, ORDER_A, piece_a)
            batchnorm(0)
            walk(dve, ORDER_B, piece_b)
            batchnorm(1)
            walk(dve, ORDER_C, piece_c)

        def free_banks(pe, b, L):
            pe.wait_ge(L.S.s["free"], (L.turn(b) * NGR if L.wide else L.head(b, 0)) + 2)

        def pe_b(pe, b, L):
            s, ff, xn = L.S.s, L.S.t["ff"], L.S.t["xn"]
            free_banks(pe, b, L)
            for k in range(L.K):
                for t in range(NTL):
                    if L is LC:
                        if k == 0 and t == 0:
                            pe.wait_ge(q["l2a"], b + 1)
                        src = oN[:, :].rearrange("p (t k f) -> p t k f", k=L.K, f=P)[:, t, k, :]
                    else:
                        pe.wait_ge(s["xn"], norm_turn(L, b) * NTL + (t + 1))
                        src = xn[:, t, :]
                    tr = nc.tensor.transpose(ps[:, hT_bank(L, k * HALVES + t // 4), (t % 4) * P:(t % 4 + 1) * P], src,
                                             identF[:, :])
                    if t % 4 == 3:
                        tr.then_inc(s["hT_ps"], 1)
            for t in range(NTL):
                pe.wait_ge(s["hinT"], hT_before(L, b) + (L.K * HALVES if L.K > 1 else t // 4 + 1))
                if t >= 2:
                    pe.wait_ge(s["hf"], L.turn(b) * (NTL + 1) + t)
                for k in range(L.K):
                    mm = nc.tensor.matmul(ps[:, proj_bank(L, t), 0:L.NC],
                                          hinT_of(L)[:, k * N + t * P:k * N + (t + 1) * P],
                                          wcat[L][:, k, :], start=(k == 0), stop=(k == L.K - 1))
                mm.then_inc(s["proj_ps"], 1)

        def pe_c(pe, b, L):
            s, ff, H2 = L.S.s, L.S.t["ff"], 2 * L.H
            fb, mb = (4, 6) if L.wide else (2, 0)
            for t in range(NTL):
                pe.wait_ge(s["f"], L.turn(b) * NTL + (t + 1))
                tr = nc.tensor.transpose(ps[0:H2, fb + t // 4, (t % 4) * P:(t % 4 + 1) * P], ff[:, 0:H2, t],
                                         identF[:, :])
                if t % 4 == 3:
                    tr.then_inc(s["frow_ps"], 1)
            pe.wait_ge(s["hf"], L.turn(b) * (NTL + 1) + (NTL + 1))
            for t in range(NTL):
                mm = nc.tensor.matmul(ps[:, mb, 0:L.H * L.W], cmean[:, :],
                                      L.S.t["hf"][:, t * L.H * L.W:(t + 1) * L.H * L.W], start=(t == 0),
                                      stop=(t == NTL - 1))
            mm.then_inc(s["mean_ps"], 1)
            pe.wait_ge(s["diag"], L.turn(b) + 1)
            nc.tensor.matmul(ps[:, mb + 1, 0:H2], ones[0:H2, :], L.S.t["diag"][0:H2, 0:H2], start=True, stop=True)\
                .then_inc(s["m2_ps"], 1)

        def pe_sums(pe, b, par, L):
            s, xv, mask = L.S.s, xp_view(L), mask_of(L, par)
            pe.wait_ge(s["mean"], L.turn(b) + 1)
            pe.wait_ge(s["m2"], L.turn(b) + 1)
            for it in range(NTL):
                if it >= 2:
                    pe.wait_ge(s["ms"], L.turn(b) * NTL + (it - 1))
                for jt in range(NTL):
                    if it == 0:
                        pe.wait_ge(s["xlo"], L.turn(b) * NTL + (jt + 1))
                    for part in range(3):
                        mm = nc.tensor.matmul(ps[:, it % 2, 0:L.H * L.W], mask[:, jt, it * P:(it + 1) * P],
                                              xv[:, jt, part, :, 1, :], start=(jt == 0 and part == 0),
                                              stop=(jt == NTL - 1 and part == 2))
                mm.then_inc(s["ms_ps"], 1)

        def pe_head(pe, b, L, h):
            s, xv, k = L.S.s, xp_view(L), 1 - h % 2
            head = L.head(b, h)
            pe.wait_ge(s["free"], head + 1)
            if h == 1:
                pe.wait_ge(s["ms"], L.turn(b) * NTL + NTL)
            for jt in range(NTL):
                pe.wait_ge(s["t"], head * NTL + (2 * NTL + jt + 1))
                for it in range(NTL):
                    for part in range(3):
                        mm = nc.tensor.matmul(
                            ps[:, 2 * k + it // 4, (it % 4) * 2 * L.W:(it % 4 + 1) * 2 * L.W],
                            T[:, jt % NT, it * P:(it + 1) * P], xv[:, jt, part, h],
                            start=(jt == 0 and it % 4 == 0 and part == 0),
                            stop=(jt == NTL - 1 and it % 4 == 3 and part == 2), skip_group_check=True)
                mm.then_inc(s["t_used"], 1)

        def pe_group(pe, b, L, g):
            s, xv, bank = L.S.s, xp_view(L), 4 + 2 * (g % 2)
            pe.wait_ge(s["free"], L.turn(b) * NGR + (g + 1))
            if g == 0:
                pe.wait_ge(s["xlo"], L.turn(b) * NTL + NTL)
            if g == 1:
                pe.wait_ge(s["mean"], L.turn(b) + 1)
                pe.wait_ge(s["m2"], L.turn(b) + 1)
            for jt in range(NTL):
                at = L.turn(b) * (NGR * NTL) + (g * NTL + jt + 1)
                for c, tile in enumerate((TW, UW)):
                    pe.wait_ge(s["tu"[c]], at if c else at + NGR * NTL)
                    for n in range(EDGES[g + 1] - EDGES[g]):
                        for part in range(3):
                            mm = nc.tensor.matmul(
                                ps[:, bank + c, n * L.W:(n + 1) * L.W], tile[:, jt, n * P:(n + 1) * P],
                                xv[:, jt, part, 0, c, :], start=(jt == 0 and n == 0 and part == 0),
                                stop=(jt == NTL - 1 and n == EDGES[g + 1] - EDGES[g] - 1 and part == 2),
                                skip_group_check=True)
                mm.then_inc(s["t_used"], 1)

        @block.tensor
        def _(pe):
            pe.wait_ge(q["cst"], 8)
            pe.wait_ge(q["wred"], 12)

            def n_piece(name, b, par, L):
                if name == "nB":
                    pe_b(pe, b, L)
                elif name == "nC":
                    pe_c(pe, b, L)
                elif name == "M":
                    pe_sums(pe, b, par, L)
                elif name[0] == "T":
                    pe_head(pe, b, L, int(name[1]))

            def piece_a(name, b, par):
                n_piece(name, b, par, LA)
                if name == "XT":
                    pe.wait_ge(q["adj_cvt"], b * NTL + (NTL + NS))
                    for t in range(NTL):
                        if t >= 4:
                            pe.wait_ge(q["mT"], b * NTL + (t - 3))
                        for it in range(NTL):
                            tr = nc.tensor.transpose(ps[:, 4 + t % 4, :].bitcast(BF16)[:, it * P:(it + 1) * P],
                                                     adj_nat[par][:, it, t * P:(t + 1) * P], identB[:, :])
                        tr.then_inc(q["mT_ps"], 1)
                elif name == "Pz":
                    pe.wait_ge(q["y1"], 2 * b + 2)
                elif name == "Xz":
                    pe.wait_ge(q["mT"], b * NTL + NTL)
                elif name == "PG":
                    pe.wait_ge(q["lo"], b + 1)
                    for rt in range(NTL):
                        if rt >= 4:
                            pe.wait_ge(q["reg"], b * NTL + (rt - 3))
                        for t in range(NTL):
                            for part in range(3):
                                mm = nc.tensor.matmul(ps[:, 4 + rt % 4, 0:P], adj_nat[par][:, t, rt * P:(rt + 1) * P],
                                                      parts[1][:, t, part, :],
                                                      start=(t == 0 and part == 0), stop=(t == NTL - 1 and part == 2))
                        mm.then_inc(q["reg_ps"], 1)
                elif name == "PC":
                    pe.wait_ge(q["reg"], b * NTL + NTL)
                    for t in range(NTL):
                        tr = nc.tensor.transpose(ps[:, 4 + t // 4, (t % 4) * P:(t % 4 + 1) * P], xnW[:, t, :],
                                                 identF[:, :])
                        if t % 4 == 3:
                            tr.then_inc(q["regT_ps"], 1)
                    for h in range(HALVES):
                        pe.wait_ge(q["regT"], 2 * b + (h + 1))
                        nc.tensor.matmul(ps[:, 6 + h, :], k1s[:, :], oW[:, h * BANK:(h + 1) * BANK],
                                         start=True, stop=True).then_inc(q["y1_ps"], 1)

            def piece_b(name, b, par):
                if name == "Ba":
                    pe.wait_ge(q["z"], b + 2)
                    for t in range(NTL):
                        mm = nc.tensor.matmul(ps[:, 4 + t // 4, (t % 4) * P:(t % 4 + 1) * P],
                                              scratch[:, t * P:(t + 1) * P], k2s[:, :], start=True, stop=True)
                        if t % 4 == 3:
                            mm.then_inc(q["G_ps"], 1)
                elif name == "Bg":
                    pe.wait_ge(q["lo"], b + (B + 1))
                    pe.wait_ge(q["mask_in"], b * 16 + 16)
                    for h in range(HALVES):
                        for t in range(NTL):
                            for part in range(3):
                                mm = nc.tensor.matmul(ps[:, 2 * par + h, :], parts[par][:, t, part, :],
                                                      maskbuf[:, par, t, h * BANK:(h + 1) * BANK],
                                                      start=(t == 0 and part == 0), stop=(t == NTL - 1 and part == 2))
                        mm.then_inc(q["y2_ps"], 1)

            def piece_c(name, b, par):
                if name == "nA":
                    pe.wait_ge(q["yn"], b + 1)
                    free_banks(pe, b, LB)
                    for t in range(NTL):
                        tr = nc.tensor.transpose(ps[:, t // 4, (t % 4) * P:(t % 4 + 1) * P],
                                                 xnN[:, t, :], identF[:, :])
                        if t % 4 == 3:
                            tr.then_inc(q["ynT_ps"], 1)
                if name == "M":
                    pe.wait_ge(q["mask_in"], b * 16 + (16 * B + 16))
                n_piece(name, b, par, LB)
                if name in ("CB", "DB"):
                    pe_b(pe, b, wide_of(name))
                elif name in ("CC", "DC"):
                    pe_c(pe, b, wide_of(name))
                elif name in ("C0", "C1", "C2", "D0", "D1", "D2"):
                    pe_group(pe, b, wide_of(name), int(name[1]))

            walk(pe, ORDER_A, piece_a)
            walk(pe, ORDER_B, piece_b)
            walk(pe, ORDER_C, piece_c)


_INS = ['x', 'adj', 'L0_gnn_W', 'L0_gnn_b', 'L0_gnn_a', 'L1_gnn_kernel_1', 'L1_gnn_bias_1', 'L1_gnn_gamma_1',
        'L1_gnn_beta_1', 'L1_gnn_kernel_2', 'L1_gnn_bias_2', 'L1_gnn_gamma_2', 'L1_gnn_beta_2', 'L2_gnn_W1',
        'L2_gnn_a1', 'L2_gnn_W2', 'L2_gnn_a2', 'L3_gnn_W', 'L3_gnn_a']


def kernel(**inputs):
    import numpy as _np
    import concourse.bacc as _bacc
    from concourse import mybir as _mybir
    from concourse.bass_utils import run_bass_kernel_spmd as _run

    nc = _bacc.Bacc("TRN2", target_bir_lowering=False, num_devices=1)
    arrays, args = {}, []
    for name in _INS:
        a = _np.ascontiguousarray(inputs[name])
        arrays[f"in_{name}"] = a
        args.append(nc.dram_tensor(f"in_{name}", a.shape, _mybir.dt.from_np(a.dtype), kind="ExternalInput").ap())
    x = inputs["x"]
    o = nc.dram_tensor("out", tuple(x.shape), _mybir.dt.float32, kind="ExternalOutput").ap()
    gnn_stack(nc, *args, o)
    r = _run(nc, [arrays], core_ids=[0])
    return r.results[0]["out"]
```

```python
from contextlib import ExitStack

import concourse.bass as bass
from concourse import mybir

ALU = mybir.AluOpType
ACT = mybir.ActivationFunctionType
AX = mybir.AxisListType
F32 = mybir.dt.float32
BF16 = mybir.dt.bfloat16
I32 = mybir.dt.int32
U8 = mybir.dt.uint8

P = 128
BANK = 512
LN_EPS = 1e-5
BN_EPS = 1e-3
SLOPE = 0.2
LIFT = 60.0
BIG = float(2 ** 60)
NT = 8
NG = 4


def gnn_stack(nc, x, adj, L0_W, L0_b, L0_a, k1, bias1, gamma1, beta1, k2, bias2, gamma2, beta2,
              W1, a1, W2, a2, L3_W, L3_a, out):
    B, N, F = x.shape
    NTL = N // P
    HALVES = N // BANK
    EDGES = [0, 3, 6, 8]
    assert F == P and NTL == 8 and HALVES == 2

    HB = B // 2

    class Layer:
        def __init__(self, name, H, D, K, act_tiles):
            self.name, self.H, self.D, self.K = name, H, D, K
            self.W = D + 1
            self.HD, self.NC = H * D, H * D + 2 * H
            self.wide = H == 1
            self.act_tiles = act_tiles

        def turn(self, b):
            return {LA: b + 0, LB: b + B, LC: 2 * b, LD: 2 * b + 1}[self]

        def head(self, b, h):
            return b * self.H + h + (B * LA.H if self is LB else 0)

    LA = Layer("l0", 4, L0_W.shape[1] // 4, 1, (1, 3, 5, 7))
    LB = Layer("l2a", W1.shape[0], W1.shape[2], 1, (1, 2, 4, 5, 6, 7))
    LC = Layer("l2b", 1, W2.shape[1], W2.shape[0] // P, ())
    LD = Layer("l3", 1, L3_W.shape[1], 1, ())
    LAYERS = [LA, LB, LC, LD]
    HM, HWM = LB.H, LB.H * LB.W
    GC = 3 * P
    NGR = len(EDGES) - 1
    U0 = 3 * NGR * NTL
    SUMS = {"M0": range(0, 4), "M1": range(4, NTL)}
    NS = 3

    ORDER_A = (("T0", 0), ("S1", 0), ("M1", 0), ("K0", 0), ("Xz", 0), ("PG", -1), ("T1", 0), ("S2", 0), ("X0", 1),
               ("K1", 0), ("T2", 0), ("PC", -1), ("S3", 0), ("X1", 1), ("K2", 0), ("T3", 0), ("nA", 1), ("Pz", -1),
               ("XT", 1), ("K3", 0), ("nF", 0), ("nB", 1), ("PA", 0), ("nC", 1), ("nm", 1), ("nD", 1), ("nE", 1),
               ("S0", 1), ("M0", 1), ("PN", 0), ("PB", 0))
    ORDER_B = (("By", 1), ("Ba", 0), ("Bl", 0), ("Bg", -1))
    ORDER_C = (("T0", 0), ("CA", -1), ("CB", -1), ("S1", 0), ("CC", -1), ("M1", 0), ("Cm", -1), ("K0", 0), ("T1", 0),
               ("CD", -1), ("S2", 0), ("K1", 0), ("T2", 0), ("CE", -1), ("S3", 0), ("K2", 0), ("c0", -1), ("T3", 0),
               ("C0", -1), ("S4", 0), ("K3", 0), ("c1", -1), ("T4", 0), ("C1", -1), ("S5", 0), ("K4", 0), ("c2", -1),
               ("T5", 0), ("C2", -1), ("S6", 0), ("K5", 0), ("T6", 0), ("CF", -1), ("DA", -1), ("S7", 0), ("DN", -1),
               ("nX", 0), ("nL", 1), ("K6", 0), ("DB", -1), ("DC", -1), ("Dm", -1), ("T7", 0), ("DD", -1), ("ny", 1),
               ("K7", 0), ("nF", 0), ("DE", -1), ("d0", -1), ("D0", -1), ("nG", 0), ("nA", 1), ("nN", 1), ("d1", -1),
               ("D1", -1), ("d2", -1), ("nB", 1), ("nC", 1), ("nm", 1), ("D2", -1), ("nD", 1), ("nE", 1), ("ML", 1),
               ("S0", 1), ("M0", 1), ("DF", -1))

    def walk(eng, order, piece):
        def iteration(b):
            for name, off in order:
                if 0 <= b + off < B:
                    piece(name, b + off, (b + off) % 2)

        iteration(-1)
        iteration(0)
        with eng.Fori(0, HB - 1) as i:
            for name, off in order:
                piece(name, i * 2 + (1 + off), 1 ^ (off & 1))
            for name, off in order:
                piece(name, i * 2 + (2 + off), off & 1)
        iteration(B - 1)
        iteration(B)

    x_t = x.rearrange("b (t p) f -> b p t f", p=P)
    out_t = out.rearrange("b (t p) f -> b p t f", p=P)
    x1_dram = nc.dram_tensor("x1_scratch", (B, P, NTL, F), F32, kind="Internal").ap()
    y1_dram = nc.dram_tensor("y1_scratch", (B, P, N), F32, kind="Internal").ap()
    y2_dram = nc.dram_tensor("y2_scratch", (B, P, N), F32, kind="Internal").ap()
    mask_dram = nc.dram_tensor("mask_scratch", (B, P, NTL, N), BF16, kind="Internal").ap()
    f1_dram = {L: nc.dram_tensor(f"f1_{L.name}", (B, L.H, N), F32, kind="Internal").ap() for L in LAYERS}

    with ExitStack() as ctx:
        def sb(name, shape, dt=F32):
            return ctx.enter_context(nc.sbuf_tensor(name, shape, dt))

        def sem(name):
            return ctx.enter_context(nc.semaphore(name))

        maskbuf = sb("maskbuf", [P, 2, NTL, N], BF16)
        tu = sb("tu", [P, NTL, N], BF16)
        TG = sb("TG", [P, NT + NG, N], BF16)
        T, G = TG[:, 0:NT], TG[:, NT:NT + NG]
        F1N = sb("F1N", [P, 2, N])
        F1W = sb("F1W", [P, 1, N])
        XpN = sb("XpN", [P, NTL * 6 * HWM], BF16)
        XpW = sb("XpW", [P, NTL * 6 * LD.W], BF16)
        scratch = sb("scratch", [P, NTL * HWM])
        hfN = sb("hfN", [P, NTL * HWM])
        hfW = sb("hfW", [P, NTL * LD.W])
        oN = sb("oN", [P, NTL * LB.HD])
        oW = sb("oW", [P, NTL * LD.HD])
        xcN, xsN, xnN, xcW, xnW = (sb(n, [P, NTL, F]) for n in ("xcN", "xsN", "xnN", "xcW", "xnW"))
        uN = sb("uN", [P, NTL * LB.W])
        uW = sb("uW", [P, NTL * LD.W])
        twf = tu[:, :, :].rearrange("p s n -> p (s n)")
        TW = twf[:, 0:NTL * GC].rearrange("p (s n) -> p s n", n=GC)
        UW = twf[:, NTL * GC:2 * NTL * GC].rearrange("p (s n) -> p s n", n=GC)
        xrN = TG[:, :, :].rearrange("p s n -> p (s n)").bitcast(F32)
        xrW = twf.bitcast(F32)
        adj_nat = (maskbuf[:, 1], tu)
        stage = XpN[:, 6 * NTL * LA.H * LA.W:].bitcast(I32)[:, 0:NS * N].rearrange("p (s n) -> p s n", s=NS)
        parts = (XpN[:, 0:3 * N].rearrange("p (t k f) -> p t k f", k=3, f=F),
                 XpW[:, 0:3 * N].rearrange("p (t k f) -> p t k f", k=3, f=F))
        identF = sb("identF", [P, P])
        identB = sb("identB", [P, P], BF16)
        ones = sb("ones", [P, P])
        cmean = sb("cmean", [P, P])
        wcat = {L: sb(f"wcat_{L.name}", [P, L.K, L.NC]) for L in LAYERS}
        bcat = sb("bcat", [P, LA.NC])
        k1s, k2s = sb("k1s", [P, P]), sb("k2s", [P, P])
        cols = sb("cols", [P, 8])
        mhalf, lneps = sb("mhalf", [P, NTL]), sb("lneps", [P, NTL])
        pad = sb("pad", [P, 1])
        outdeg, indeg, rin, empty = (sb(n, [P, NTL]) for n in ("outdeg", "indeg", "rin", "empty"))
        empty_all = sb("empty_all", [P, B, NTL])
        rin_all = sb("rin_all", [P, B, NTL])
        bst = [sb(f"bst{n}", [P, B * HALVES, 6]) for n in range(2)]
        bmv, bsc = sb("bmv", [P, 2, 2]), sb("bsc", [P, 2, 4])
        ps = ctx.enter_context(nc.psum_tensor("ps", [P, 8, BANK], F32))

        class Stream:
            def __init__(self, c, bank, H, **named):
                self.c, self.bank = c, bank
                self.t = dict(named)
                self.t.update({n: sb(f"{n}{c}", [P, H, NTL]) for n in ("g2", "nf2", "nbf2", "cpos", "crow")})
                self.t.update({n: sb(f"{n}{c}", [P, NTL]) for n in ("nm", "vpe", "rstd", "nmr")})
                self.t.update(ff=sb(f"ff{c}", [P, 2 * H, NTL]), bb=sb(f"bb{c}", [P, 2, H, NTL]),
                              st=sb(f"st{c}", [P, NTL, 6]), mv=sb(f"mv{c}", [P, NTL, 2]), mx=sb(f"mx{c}", [P, 1]),
                              diag=sb(f"diag{c}", [P, 2 * H]), m2=sb(f"m2{c}", [P, 2 * H]),
                              den=sb(f"den{c}", [P, 2, NTL]), empty=sb(f"empty{c}", [P, NTL]),
                              meanb=sb(f"meanb{c}", [P, LB.H * LB.W if c == "N" else LD.W]))
                self.s = {n: sem(f"{n}_{c}") for n in (
                    "proj_ps", "f", "hf", "frow_ps", "frow", "frow_out", "f1_0", "mean_ps", "mean", "mx", "diag",
                    "m2_ps", "m2", "g2", "c0", "c1", "expo", "xf", "xhi", "xr", "xmid", "xlo", "fin", "emin",
                    "eexp", "elu", "t", "t_used", "cmb", "free", "hT_ps", "hinT",
                    "stats", "moments", "nmr1", "pow", "rstd", "xn")}
                self.s.update({n: sem(n) for n in (("f1_1", "g", "ms_ps", "ms") if c == "N" else ("u",))})

        SN = Stream("N", 0, LB.H, hf=hfN, o=oN, u=uN, Xp=XpN, xr=xrN, xn=xnN)
        SW = Stream("W", 4, 1, hf=hfW, o=oW, u=uW, Xp=XpW, xr=xrW, xn=xnW)
        for L in LAYERS:
            L.S = SW if L.wide else SN

        atmp = uW[:, 0:512]
        abc = {LA: scratch[:, 1024:1088], LB: scratch[:, 0:512], LC: scratch[:, 512:768], LD: scratch[:, 768:1024]}
        q = {n: sem(n) for n in (
            "w_in", "sp_waits", "cst", "wprod", "wred", "adj_in0", "adj_in1", "adj_in2", "adj_cvt", "mT_ps", "mT",
            "mask_out", "mask_in", "deg0", "deg", "x_in", "x1", "x1_out",
            "hi", "r1", "mid", "lo", "reg_ps", "reg",
            "regT_ps", "regT", "y1_ps", "y1", "y1s", "y1_out", "bag0", "bpow0", "bs0", "bt0", "bag1", "bpow1", "bs1",
            "bt1", "y1_in", "z", "G_ps", "Gf", "y2_ps", "y2", "y2s", "y2_out",
            "y2_in", "x1_in", "yn", "ynT_ps", "x2", "emp", "empW", "xsum", "x3", "out_x", "out")}

        block = ctx.enter_context(nc.Block())

        def hinT_of(L):
            if L.wide:
                return XpW[:, 0:2 * L.K * N].bitcast(F32)
            return scratch[:, L.H * L.W * NTL:][:, 0:N] if L is LA else scratch[:, 0:N]

        def frow_of(L):
            return uW[:, 0:N] if L.wide else hfN[:, L.H * L.W * NTL:][:, 0:N] if L is LA else scratch[:, N:2 * N]

        def ms_view(L):
            return scratch[:, 0:NTL * L.H * L.W].rearrange("p (t h w) -> p t h w", h=L.H, w=L.W)

        def hf_view(L):
            return L.S.t["hf"][:, 0:NTL * L.H * L.W].rearrange("p (t h w) -> p t h w", h=L.H, w=L.W)

        def o_view(L):
            return L.S.t["o"][:, 0:NTL * L.HD].rearrange("p (t h d) -> p t h d", h=L.H, d=L.D)

        def xp_view(L):
            return L.S.t["Xp"][:, 0:NTL * 6 * L.H * L.W].rearrange("p (t k h c w) -> p t k h c w", k=3, h=L.H, c=2,
                                                                 w=L.W)

        def xt_view(L, t):
            n = 2 * L.H * L.W
            return L.S.t["xr"][:, t * n:(t + 1) * n].rearrange("p (h c w) -> p h c w", c=2, w=L.W)

        def mask_of(L, par):
            return maskbuf[:, 0] if L is LA else maskbuf[:, par]

        def x_of(par):
            return (xcN, xsN)[par]

        def y1_buf(par):
            return hfN[:, par * N:(par + 1) * N]

        def norm_turn(L, b):
            return b + 0 if L is LA or L is None else b + B

        def ms_bank(it):
            return it if it < 4 else it % 2

        def ones_before(L, t):
            return sum(1 for a in L.act_tiles if a < t)

        def wide_of(name):
            return LC if name[0] in "Cc" else LD

        @block.sync
        def _(sp):
            for dst, src in (
                (wcat[LA][:, 0, 0:LA.HD], L0_W), (k1s[:, :], k1), (k2s[:, :], k2),
                (wcat[LB][:, 0, 0:LB.HD].rearrange("p (h d) -> p h d", h=LB.H), W1.rearrange("h f d -> f h d")),
                (wcat[LC][:, :, 0:LC.HD], W2.rearrange("(k p) n -> p k n", p=P)),
                (wcat[LD][:, 0, 0:LD.HD], L3_W),
                (bcat[:, 0:LA.HD], L0_b.rearrange("(a n) -> a n", a=1).to_broadcast((P, LA.HD))),
                (abc[LA], L0_a.rearrange("n a -> a n").to_broadcast((P, 64))),
                (abc[LB], a1.rearrange("(a h) n -> a (h n)", a=1).to_broadcast((P, 512))),
                (abc[LC], a2.rearrange("(a n) -> a n", a=1).to_broadcast((P, 256))),
                (abc[LD], L3_a.rearrange("(a n) -> a n", a=1).to_broadcast((P, 256))),
                *((cols[:, n:n + 1], v.rearrange("(p a) -> p a", a=1))
                  for n, v in enumerate((bias1, gamma1, beta1, bias2, gamma2, beta2))),
            ):
                sp.dma_start(dst, src).then_inc(q["w_in"], 16)

            def wait(s, value):
                sp.wait_ge(s, value)
                sp.sem_inc(q["sp_waits"], 1)

            def store_f_rows(L, b):
                s = L.S.s
                wait(s["frow"], L.turn(b) + 1)
                sp.dma_start(f1_dram[L][b], frow_of(L)[0:L.H, :]).then_inc(s["frow_out"], 16)
                wait(s["frow_out"], L.turn(b) * 16 + 16)

            def load_f1(L, b, h):
                s = L.S.s
                if L.wide:
                    wait(s["t"], L.turn(b) * (NGR * NTL) + NGR * NTL)
                    sp.dma_start(F1W[:, 0, :], f1_dram[L][b].to_broadcast((P, N))).then_inc(s["f1_0"], 16)
                else:
                    wait(s["t"], L.head(b, h) * NTL + NTL)
                    sp.dma_start(F1N[:, h % 2, :], f1_dram[L][b, h:h + 1, :].to_broadcast((P, N)))\
                        .then_inc(s[f"f1_{h % 2}"], 16)

            def piece_a(name, b, par):
                if name in ("X0", "X1"):
                    for t in range(*((0, 4) if name == "X0" else (4, NTL))):
                        wait(q["adj_cvt"], b * NTL + (t + 1))
                        sp.dma_start(stage[:, (t % NS), :], adj[b, t * P:(t + 1) * P, :])\
                            .then_inc(q[f"adj_in{t % NS}"], 16)
                elif name == "nA":
                    sp.dma_start(x_of(par)[:, :, :], x_t[b]).then_inc(q["x_in"], 16)
                elif name == "nC":
                    store_f_rows(LA, b)
                    load_f1(LA, b, 0)
                elif name[0] == "S" and int(name[1]) + 1 < LA.H:
                    load_f1(LA, b, int(name[1]) + 1)
                elif name == "XT":
                    wait(q["mT"], b * NTL + NTL)
                    sp.dma_start(mask_dram[b], maskbuf[:, 0]).then_inc(q["mask_out"], 16)
                elif name == "PA":
                    wait(q["x1"], b + 1)
                    sp.dma_start(x1_dram[b], xcW[:, :, :]).then_inc(q["x1_out"], 16)
                elif name == "PC":
                    wait(q["y1"], 2 * b + 2)
                    sp.dma_start(y1_dram[b], hfW[:, 0:N]).then_inc(q["y1_out"], 16)

            def piece_b(name, b, par):
                if name == "By":
                    wait(q["y1_in"], b * 16 + 16)
                    wait(q["z"], b + 1)
                    sp.dma_start(y1_buf(par), y1_dram[b]).then_inc(q["y1_in"], 16)
                elif name == "Bl":
                    wait(q["y2s"], b * 2 + 2)
                    sp.dma_start(maskbuf[:, par], mask_dram[b]).then_inc(q["mask_in"], 16)
                    wait(q["mask_in"], b * 16 + 16)
                elif name == "Bg":
                    wait(q["y2"], 2 * b + 2)
                    sp.dma_start(y2_dram[b], hfW[:, 0:N]).then_inc(q["y2_out"], 16)

            def piece_c(name, b, par):
                if name == "nL":
                    wait(q["xsum"], b + 1)
                    sp.dma_start(xnN[:, :, :].rearrange("p t f -> p (t f)"), y2_dram[b]).then_inc(q["y2_in"], 16)
                    sp.dma_start(xcN[:, :, :], x1_dram[b]).then_inc(q["x1_in"], 16)
                elif name == "nC":
                    store_f_rows(LB, b)
                    load_f1(LB, b, 0)
                elif name[0] == "S" and int(name[1]) + 1 < LB.H:
                    load_f1(LB, b, int(name[1]) + 1)
                elif name == "ML":
                    wait(SW.s["u"], (b * 2 - 2) * (NGR * NTL) + U0)
                    sp.dma_start(maskbuf[:, par], mask_dram[b]).then_inc(q["mask_in"], 16)
                elif name in ("CC", "DC"):
                    store_f_rows(wide_of(name), b)
                    load_f1(wide_of(name), b, 0)
                elif name == "DF":
                    wait(q["x3"], b + 3)
                    sp.dma_start(out_t[b], xcW[:, :, :]).then_inc(q["out"], 16)

            walk(sp, ORDER_A, piece_a)
            wait(q["y1_out"], B * 16 + 16)
            wait(q["x1_out"], B * 16 + 16)
            wait(q["mask_out"], B * 16 + 16)
            walk(sp, ORDER_B, piece_b)
            wait(q["y2_out"], B * 16 + 16)
            walk(sp, ORDER_C, piece_c)
            sp.wait_ge(q["out"], B * 16 + 16)

        def pool_rstd(pool, S, turn):
            s, t = S.s, S.t
            pool.wait_ge(s["moments"], turn * NTL + NTL)
            nc.gpsimd.tensor_tensor(t["vpe"][:, :], t["mv"][:, :, 1], lneps[:, :], ALU.add).then_inc(s["nmr1"], 1)
            nc.gpsimd.tensor_scalar(t["nm"][:, :], t["mv"][:, :, 0], -1.0, None, ALU.mult).then_inc(s["nmr1"], 1)
            pool.wait_ge(s["nmr1"], turn * 2 + 2)
            nc.gpsimd.tensor_tensor(t["rstd"][:, :], t["vpe"][:, :], mhalf[:, :], ALU.pow).then_inc(s["pow"], 1)
            pool.wait_ge(s["pow"], turn + 1)
            nc.gpsimd.tensor_tensor(t["nmr"][:, :], t["nm"][:, :], t["rstd"][:, :], ALU.mult).then_inc(s["rstd"], 1)

        def pool_parts(pool, b, L):
            s = L.S.s
            for t in range(NTL):
                pool.wait_ge(s["xhi"], L.turn(b) * NTL + (t + 1))
                nc.gpsimd.tensor_tensor(xt_view(L, t), xt_view(L, t), xp_view(L)[:, t, 0], ALU.subtract)\
                    .then_inc(s["xr"], 1)
            if L is LC:
                for t in range(NTL):
                    pool.wait_ge(s["xmid"], L.turn(b) * NTL + (t + 1))
                    nc.gpsimd.tensor_tensor(xp_view(L)[:, t, 2], xt_view(L, t), xp_view(L)[:, t, 1],
                                            ALU.subtract).then_inc(s["xlo"], 1)

        def pool_complement(pool, b, par, L, g):
            s = L.S.s
            n = (EDGES[g + 1] - EDGES[g]) * P
            for jt in range(NTL):
                at = L.turn(b) * (NGR * NTL) + (g * NTL + jt + 1)
                pool.wait_ge(s["t"], at + NGR * NTL)
                pool.wait_ge(s["t_used"], at)
                nc.gpsimd.tensor_tensor(UW[:, jt, 0:n], mask_of(L, par)[:, jt, EDGES[g] * P:EDGES[g + 1] * P],
                                        TW[:, jt, 0:n], ALU.subtract).then_inc(s["u"], 1)

        @block.gpsimd
        def _(pool):
            pool.memset(identF[:, :], 0.0).then_inc(q["cst"], 1)
            pool.memset(ones[:, :], 1.0).then_inc(q["cst"], 1)
            pool.memset(cmean[:, :], 1.0 / N).then_inc(q["cst"], 1)
            pool.memset(mhalf[:, :], -0.5).then_inc(q["cst"], 1)
            pool.memset(lneps[:, :], LN_EPS).then_inc(q["cst"], 1)
            pool.memset(cols[:, 6:7], LIFT).then_inc(q["cst"], 1)
            pool.memset(cols[:, 7:8], -1.0).then_inc(q["cst"], 1)
            pool.wait_ge(q["cst"], 7)
            pool.affine_select(out=identF[:, :], in_=identF[:, :], compare_op=ALU.not_equal, fill=1.0, base=0,
                               pattern=[[-1, P]], channel_multiplier=1).then_inc(q["cst"], 1)
            pool.wait_ge(q["cst"], 8)
            pool.tensor_copy(identB[:, :], identF[:, :]).then_inc(q["cst"], 1)

            def piece_a(name, b, par):
                if name == "nA":
                    pool_rstd(pool, SN, norm_turn(LA, b))
                elif name == "nD":
                    pool_parts(pool, b, LA)
                elif name == "PA":
                    pool_rstd(pool, SW, norm_turn(None, b))

            def piece_c(name, b, par):
                if name == "nA":
                    pool_rstd(pool, SN, norm_turn(LB, b))
                elif name == "nD":
                    pool_parts(pool, b, LB)
                elif name == "DA":
                    pool_rstd(pool, SW, norm_turn(LD, b))
                elif name == "nX":
                    pool.wait_ge(q["out_x"], b + 1)
                    pool.wait_ge(SN.s["xn"], norm_turn(LB, b) * NTL + NTL)
                    nc.gpsimd.tensor_tensor(xsN[:, :, :], xnN[:, :, :], xcN[:, :, :], ALU.add).then_inc(q["xsum"], 1)
                elif name in ("CD", "DD"):
                    pool_parts(pool, b, wide_of(name))
                elif name in ("c0", "c1", "c2", "d0", "d1", "d2"):
                    pool_complement(pool, b, par, wide_of(name), int(name[1]))

            walk(pool, ORDER_A, piece_a)
            for n in range(2):
                pool.wait_ge(q[f"bag{n}"], 2)
                pool.tensor_tensor(bsc[:, n, 1:2], bsc[:, n, 0:1], mhalf[:, 0:1], ALU.pow)\
                    .then_inc(q[f"bpow{n}"], 1)
            walk(pool, ORDER_C, piece_c)

        def act_normalise(act, S, turn, xc):
            s, xn, rstd, nmr = S.s, *(S.t[n] for n in ("xn", "rstd", "nmr"))
            act.wait_ge(s["rstd"], turn + 1)
            for t in range(NTL):
                nc.scalar.activation(xn[:, t, :], xc[:, t, :], ACT.Relu, scale=rstd[:, t:t + 1],
                                     bias=nmr[:, t:t + 1]).then_inc(s["xn"], 1)

        def act_b(act, b, L):
            s, bank = L.S.s, L.S.bank
            for k in range(L.K):
                for h in range(HALVES):
                    n = k * HALVES + h
                    act.wait_ge(s["hT_ps"], hT_before(L, b) + (n + 1))
                    if L is LC:
                        nc.scalar.activation(hinT_of(L)[:, n * BANK:(n + 1) * BANK], ps[:, hT_bank(L, n), :],
                                             ACT.Identity, bias=cols[:, 7:8]).then_inc(s["hinT"], 1)
                    else:
                        nc.scalar.activation(hinT_of(L)[:, n * BANK:(n + 1) * BANK], ps[:, hT_bank(L, n), :],
                                             ACT.Relu).then_inc(s["hinT"], 1)

        def hT_before(L, b):
            return HALVES * L.turn(b) if not L.wide else b * (HALVES * (LC.K + LD.K)) + (HALVES * LC.K if L is LD else 0)

        def hT_bank(L, n):
            return 4 + n if L.wide else 2 + n

        def act_c(act, b, L):
            s, t, H2 = L.S.s, L.S.t, 2 * L.H
            fb = 4 if L.wide else 2
            act.wait_ge(s["frow_ps"], HALVES * L.turn(b) + HALVES)
            nc.scalar.activation(frow_of(L)[0:H2, :].rearrange("p (a n) -> p a n", a=2), ps[0:H2, fb:fb + 2, :],
                                 ACT.Copy).then_inc(s["frow"], 1)
            act.wait_ge(s["mean_ps"], L.turn(b) + 1)
            nc.scalar.activation(t["meanb"][:, 0:L.H * L.W], ps[:, L.S.bank + (2 if L.wide else 0), 0:L.H * L.W],
                                 ACT.Copy).then_inc(s["mean"], 1)

        def act_m(act, b, L):
            s, t = L.S.s, L.S.t
            act.wait_ge(s["g2"], L.turn(b) + 1)
            nc.scalar.activation(t["bb"][:, 0, 0:L.H, :], t["g2"][:, 0:L.H, :], ACT.Exp, bias=cols[:, 6:7])\
                .then_inc(s["expo"], 1)
            nc.scalar.activation(t["bb"][:, 1, 0:L.H, :], t["g2"][:, 0:L.H, :], ACT.Exp, scale=SLOPE)\
                .then_inc(s["expo"], 1)
            act.wait_ge(s["c1"], L.turn(b) + 1)
            nc.scalar.activation(t["crow"][:, 0:L.H, :], t["cpos"][:, 0:L.H, :], ACT.Exp, scale=SLOPE - 1.0,
                                 bias=cols[:, 6:7]).then_inc(s["expo"], 1)

        def act_d(act, b, L):
            s = L.S.s
            for t in range(NTL):
                act.wait_ge(s["xf"], L.turn(b) * NTL + (t + 1))
                nc.scalar.activation(xp_view(L)[:, t, 0], xt_view(L, t), ACT.Copy).then_inc(s["xhi"], 1)

        def act_e(act, b, L):
            s = L.S.s
            for t in range(NTL):
                act.wait_ge(s["xr"], L.turn(b) * NTL + (t + 1))
                nc.scalar.activation(xp_view(L)[:, t, 1], xt_view(L, t), ACT.Copy).then_inc(s["xmid"], 1)

        def act_sums(act, b, L, tiles):
            s = L.S.s
            act.wait_ge(s["frow_out"], L.turn(b) * 16 + 16)
            for it in tiles:
                act.wait_ge(s["ms_ps"], L.turn(b) * NTL + (it + 1))
                nc.scalar.activation(ms_view(L)[:, it], ps[:, ms_bank(it), 0:L.H * L.W].rearrange(
                    "p (h w) -> p h w", h=L.H), ACT.Copy).then_inc(s["ms"], 1)

        def act_signs(act, b, L, h):
            s, na = L.S.s, len(L.act_tiles)
            act.wait_ge(s[f"f1_{h % 2}"], f1_count(L, b, h))
            if h == 0:
                act.wait_ge(s["xlo"], L.turn(b) * NTL + NTL)
            for n, jt in enumerate(L.act_tiles):
                c = (h % 2) * na + n
                back = (c - NG) % (2 * na)
                act.wait_ge(s["t"], L.head(b, h - h % 2) * NTL + (
                    2 * NTL + (back // na) * NTL + L.act_tiles[back % na] + 1 - (2 * NTL if c < NG else 0)))
                nc.scalar.activation(G[:, c % NG, :], F1N[:, h % 2, :], ACT.Relu, scale=-BIG,
                                     bias=L.S.t["nbf2"][:, h, jt:jt + 1]).then_inc(s["g"], 1)

        def f1_count(L, b, h):
            return (b * (L.H // 2) + (h // 2 + 1 + (B * LA.H // 2 if L is LB else 0))) * 16

        def elu_turn(L, b):
            return b + 0 if L is LB else L.turn(b)

        def act_elu(act, b, L):
            act.wait_ge(L.S.s["emin"], elu_turn(L, b) + 1)
            hf = L.S.t["hf"]
            nc.scalar.activation(hf[:, 0:NTL * L.HD], hf[:, 0:NTL * L.HD], ACT.Exp).then_inc(L.S.s["eexp"], 1)

        @block.scalar
        def _(act):
            act.wait_ge(q["cst"], 9)
            act.sem_inc(q["adj_cvt"], NS)
            act.sem_inc(q["z"], 2)

            def n_piece(name, b, par, L):
                if name == "nB":
                    act_b(act, b, L)
                elif name == "nC":
                    act_c(act, b, L)
                elif name == "nm":
                    act_m(act, b, L)
                elif name == "nD":
                    act_d(act, b, L)
                elif name == "nE":
                    act_e(act, b, L)
                elif name in ("M0", "M1"):
                    act_sums(act, b, L, SUMS[name])
                elif name[0] == "S":
                    act_signs(act, b, L, int(name[1]))

            def piece_a(name, b, par):
                n_piece(name, b, par, LA)
                if name in ("X0", "X1"):
                    for t in range(*((0, 4) if name == "X0" else (4, NTL))):
                        k = t % NS
                        per = len(range(k, NTL, NS))
                        act.wait_ge(q[f"adj_in{k}"], b * (16 * per) + (16 * (t // NS) + 16))
                        nc.scalar.activation(adj_nat[par][:, t, :], stage[:, k, :], ACT.Copy,
                                             accum_out=outdeg[:, t:t + 1]).then_inc(q["adj_cvt"], 1)
                elif name == "XT":
                    act.wait_ge(q["mask_out"], b * 16 + 16)
                    for t in range(NTL):
                        act.wait_ge(q["mT_ps"], b * NTL + (t + 1))
                        nc.scalar.activation(maskbuf[:, 0, t, :], ps[:, 4 + t % 4, :].bitcast(BF16), ACT.Copy,
                                             accum_out=indeg[:, t:t + 1]).then_inc(q["mT"], 1)
                elif name == "PN":
                    act_normalise(act, SW, norm_turn(None, b), xcW)
                elif name == "PB":
                    act.wait_ge(SW.s["xn"], norm_turn(None, b) * NTL + NTL)
                    nc.scalar.activation(parts[1][:, :, 0, :], xnW[:, :, :], ACT.Relu).then_inc(q["hi"], 1)
                    act.wait_ge(q["r1"], b + 1)
                    nc.scalar.activation(parts[1][:, :, 1, :], oW[:, :].rearrange("p (t f) -> p t f", f=F), ACT.Copy)\
                        .then_inc(q["mid"], 1)
                elif name == "PG":
                    for t in range(NTL):
                        act.wait_ge(q["reg_ps"], b * NTL + (t + 1))
                        nc.scalar.activation(xnW[:, t, :], ps[:, 4 + t % 4, 0:P], ACT.Copy,
                                             scale=rin_all[:, b, t:t + 1]).then_inc(q["reg"], 1)
                elif name == "PC":
                    for h in range(HALVES):
                        act.wait_ge(q["regT_ps"], 2 * b + (h + 1))
                        nc.scalar.activation(oW[:, h * BANK:(h + 1) * BANK], ps[:, 4 + h, :], ACT.Copy)\
                            .then_inc(q["regT"], 1)
                    for h in range(HALVES):
                        act.wait_ge(q["y1_ps"], 2 * b + (h + 1))
                        if h == 0:
                            act.wait_ge(q["y1_out"], b * 16 + 16)
                        nc.scalar.activation(hfW[:, h * BANK:(h + 1) * BANK], ps[:, 6 + h, :], ACT.Identity,
                                             bias=cols[:, 0:1]).then_inc(q["y1"], 1)

            def piece_b(name, b, par):
                if name == "Ba":
                    act.wait_ge(q["y1_in"], b * 16 + 32)
                    nc.scalar.activation(scratch[:, 0:N], y1_buf(par), ACT.Identity, scale=bsc[:, 0, 2:3],
                                         bias=bsc[:, 0, 3:4]).then_inc(q["z"], 1)
                    for t in range(NTL):
                        if t % 4 == 0:
                            act.wait_ge(q["G_ps"], 2 * b + (t // 4 + 1))
                        nc.scalar.activation(xnN[:, t, :], ps[:, 4 + t // 4, (t % 4) * P:(t % 4 + 1) * P], ACT.Copy,
                                             scale=rin_all[:, b, t:t + 1]).then_inc(q["Gf"], 1)
                    act.wait_ge(q["Gf"], b * NTL + NTL)
                    nc.scalar.activation(parts[par][:, :, 0, :], xnN[:, :, :], ACT.Copy).then_inc(q["hi"], 1)
                    act.wait_ge(q["r1"], b + (B + 1))
                    nc.scalar.activation(parts[par][:, :, 1, :], oN[:, 0:N].rearrange("p (t f) -> p t f", f=F),
                                         ACT.Copy).then_inc(q["mid"], 1)
                elif name == "Bg":
                    act.wait_ge(q["y2_out"], b * 16 + 16)
                    act.wait_ge(q["y2s"], 2 * b + 4)
                    for h in range(HALVES):
                        act.wait_ge(q["y2_ps"], 2 * b + (h + 1))
                        nc.scalar.activation(hfW[:, h * BANK:(h + 1) * BANK], ps[:, 2 * par + h, :], ACT.Identity,
                                             bias=cols[:, 3:4]).then_inc(q["y2"], 1)

            def piece_c(name, b, par):
                if name == "ny":
                    act.wait_ge(q["y2_in"], b * 16 + 16)
                    xf = xnN[:, :, :].rearrange("p t f -> p (t f)")
                    nc.scalar.activation(xf, xf, ACT.Identity, scale=bsc[:, 1, 2:3], bias=bsc[:, 1, 3:4])\
                        .then_inc(q["yn"], 1)
                n_piece(name, b, par, LB)
                if name == "nN":
                    act_normalise(act, SN, norm_turn(LB, b), xcN)
                elif name == "DN":
                    act_normalise(act, SW, norm_turn(LD, b), xcW)
                elif name == "nG":
                    act_elu(act, b, LB)
                elif name in ("CB", "DB"):
                    act_b(act, b, wide_of(name))
                elif name in ("CC", "DC"):
                    act_c(act, b, wide_of(name))
                elif name in ("Cm", "Dm"):
                    act_m(act, b, wide_of(name))
                elif name in ("CD", "DD"):
                    act_d(act, b, wide_of(name))
                elif name in ("CE", "DE"):
                    act_e(act, b, wide_of(name))
                elif name in ("CF", "DF"):
                    act_elu(act, b, wide_of(name))

            walk(act, ORDER_A, piece_a)
            act.wait_ge(q["bt0"], 1)
            walk(act, ORDER_B, piece_b)
            act.wait_ge(q["bt1"], 1)
            walk(act, ORDER_C, piece_c)

        def dve_norm(dve, S, turn, xc):
            dve_stats(dve, S, turn, xc)
            dve_normalise(dve, S, turn, xc)

        def dve_stats(dve, S, turn, xc):
            s, st, mv = S.s, *(S.t[n] for n in ("st", "mv"))
            for t in range(NTL):
                nc.vector.bn_stats(st[:, t, :], xc[:, t, :]).then_inc(s["stats"], 1)
            dve.wait_ge(s["stats"], turn * NTL + NTL)
            nc.vector.memset(pad[:, :], 0.0)
            for t in range(NTL):
                nc.vector.bn_aggr(mv[:, t, :], st[:, t, :]).then_inc(s["moments"], 1)

        def dve_normalise(dve, S, turn, xc):
            s, xn, rstd, nmr = S.s, *(S.t[n] for n in ("xn", "rstd", "nmr"))
            dve.wait_ge(s["rstd"], turn + 1)
            for t in range(NTL):
                nc.vector.tensor_scalar(xn[:, t, :], xc[:, t, :], rstd[:, t:t + 1], nmr[:, t:t + 1],
                                        ALU.mult, ALU.add).then_inc(s["xn"], 1)

        def dve_b(dve, b, L):
            s, H, H2, bank, ff = L.S.s, L.H, 2 * L.H, L.S.bank, L.S.t["ff"]
            hv = hf_view(L)
            nc.vector.memset(hv[:, :, :, L.D:L.W], 1.0).then_inc(s["hf"], 1)
            for t in range(NTL):
                dve.wait_ge(s["proj_ps"], L.turn(b) * NTL + (t + 1))
                pj = ps[:, proj_bank(L, t), :]
                src = pj[:, 0:L.HD].rearrange("p (h d) -> p h d", h=H)
                if L is LA:
                    nc.vector.tensor_tensor(ff[:, 0:H2, t], pj[:, L.HD:L.NC], bcat[:, L.HD:L.NC], ALU.add)\
                        .then_inc(s["f"], 1)
                    nc.vector.tensor_tensor(hv[:, t, :, 0:L.D], src,
                                            bcat[:, 0:L.HD].rearrange("p (h d) -> p h d", h=H), ALU.add)\
                        .then_inc(s["hf"], 1)
                else:
                    nc.vector.tensor_copy(ff[:, 0:H2, t], pj[:, L.HD:L.NC]).then_inc(s["f"], 1)
                    nc.vector.tensor_copy(hv[:, t, :, 0:L.D], src).then_inc(s["hf"], 1)

        def proj_bank(L, t):
            return (6 if L.wide else 0) + t % 2

        def dve_c(dve, b, L):
            s, H, H2 = L.S.s, L.H, 2 * L.H
            mx, diag = L.S.t["mx"], L.S.t["diag"]
            dve.wait_ge(s["frow"], L.turn(b) + 1)
            nc.vector.tensor_reduce(mx[0:H2, :], frow_of(L)[0:H2, :], axis=AX.X, op=ALU.max).then_inc(s["mx"], 1)
            dve.wait_ge(s["mx"], L.turn(b) + 1)
            nc.vector.tensor_scalar(diag[0:H2, 0:H2], identF[0:H2, 0:H2], mx[0:H2, :], None, ALU.mult)\
                .then_inc(s["diag"], 1)

        def dve_m(dve, b, L):
            s, H, H2 = L.S.s, L.H, 2 * L.H
            m2, g2, cpos, nf2, nbf2, ff = (L.S.t[n] for n in ("m2", "g2", "cpos", "nf2", "nbf2", "ff"))
            dve.wait_ge(s["m2_ps"], L.turn(b) + 1)
            nc.vector.tensor_copy(m2[:, 0:H], ps[:, 7 if L.wide else 1, H:H2]).then_inc(s["m2"], 1)
            dve.wait_ge(s["m2"], L.turn(b) + 1)
            m2v = m2[:, 0:H].unsqueeze(2).to_broadcast((P, H, NTL))
            nc.vector.tensor_tensor(g2[:, 0:H, :], ff[:, H:H2, :], m2v, ALU.subtract).then_inc(s["g2"], 1)
            nc.vector.tensor_tensor(cpos[:, 0:H, :], ff[:, 0:H, :], m2v, ALU.add).then_inc(s["c0"], 1)
            nc.vector.tensor_scalar(nf2[:, 0:H, :], ff[:, H:H2, :], -1.0, None, ALU.mult).then_inc(s["c0"], 1)
            nc.vector.tensor_scalar(nbf2[:, 0:H, :], ff[:, H:H2, :], -BIG, None, ALU.mult).then_inc(s["c0"], 1)
            dve.wait_ge(s["c0"], 3 * L.turn(b) + 3)
            nc.vector.tensor_scalar(cpos[:, 0:H, :], cpos[:, 0:H, :], 0.0, None, ALU.max).then_inc(s["c1"], 1)

        def dve_d(dve, b, L):
            s, H, bb, hv = L.S.s, L.H, L.S.t["bb"], hf_view(L)
            dve.wait_ge(s["expo"], 3 * L.turn(b) + 3)
            dve.wait_ge(s["hf"], L.turn(b) * (NTL + 1) + (NTL + 1))
            for t in range(NTL):
                nc.vector.tensor_tensor(
                    xt_view(L, t), hv[:, t].unsqueeze(2).to_broadcast((P, H, 2, L.W)),
                    bb[:, :, 0:H, t].rearrange("p c h -> p h c").unsqueeze(3).to_broadcast((P, H, 2, L.W)),
                    ALU.mult).then_inc(s["xf"], 1)

        def dve_e(dve, b, L):
            s = L.S.s
            for t in range(NTL):
                dve.wait_ge(s["xmid"], L.turn(b) * NTL + (t + 1))
                nc.vector.tensor_tensor(xp_view(L)[:, t, 2], xt_view(L, t), xp_view(L)[:, t, 1], ALU.subtract)\
                    .then_inc(s["xlo"], 1)

        def dve_divide(dve, L, h, src, step):
            s, den, empty = L.S.s, L.S.t["den"], L.S.t["empty"]
            nc.vector.tensor_tensor(den[:, 0, :], src[:, :, L.D], empty[:, :], ALU.add).then_inc(s["cmb"], 1)
            dve.wait_ge(s["cmb"], step + 1)
            nc.vector.reciprocal(den[:, 1, :], den[:, 0, :]).then_inc(s["cmb"], 1)
            dve.wait_ge(s["cmb"], step + 2)
            nc.vector.tensor_tensor(o_view(L)[:, :, h, :], src[:, :, 0:L.D],
                                    den[:, 1, :].unsqueeze(2).to_broadcast((P, NTL, L.D)), ALU.mult)\
                .then_inc(s["cmb"], 1)

        def dve_combine(dve, b, L, h):
            s, u, k = L.S.s, L.S.t["u"], 1 - h % 2
            head = L.head(b, h)
            step = head * 6 + 1
            dve.wait_ge(s["t_used"], head * NTL + (NT + NTL))
            dve.wait_ge(s["ms"], L.turn(b) * NTL + NTL)
            acc = ps[:, 2 * k:2 * k + 2, 0:4 * 2 * L.W].rearrange("p a (t c w) -> p a t c w", c=2, w=L.W)
            uv = u[:, 0:NTL * L.W].rearrange("p (a t w) -> p a t w", a=2, w=L.W)
            ut = u[:, 0:NTL * L.W].rearrange("p (t w) -> p t w", w=L.W)
            dve.wait_ge(s["cmb"], step)
            for a in range(2):
                nc.vector.tensor_tensor(uv[:, a], ms_view(L)[:, 4 * a:4 * a + 4, h, :], acc[:, a, :, 1, :],
                                        ALU.subtract).then_inc(s["cmb"], 1)
            dve.wait_ge(s["cmb"], step + 2)
            nc.vector.tensor_tensor(ut, ut, L.S.t["crow"][:, h, :].unsqueeze(2).to_broadcast((P, NTL, L.W)), ALU.mult)\
                .then_inc(s["cmb"], 1)
            dve.wait_ge(s["cmb"], step + 3)
            nc.vector.tensor_tensor(uv, uv, acc[:, :, :, 0, :], ALU.add).then_inc(s["free"], 1)
            dve.wait_ge(s["free"], head + 3)
            dve_divide(dve, L, h, ut, step + 3)

        def dve_thresholds(dve, b, par, L, h):
            s, na, k = L.S.s, len(L.act_tiles), h % 2
            head, mask = L.head(b, h), mask_of(L, par)
            dve.wait_ge(s[f"f1_{k}"], f1_count(L, b, h))
            if h == 0:
                dve.wait_ge(s["xlo"], L.turn(b) * NTL + NTL)
            for jt in range(NTL):
                dve.wait_ge(s["t_used"], head * NTL + (jt + 1))
                if jt in L.act_tiles:
                    n = ones_before(L, jt)
                    signs = (n + 1) - (B * LA.H * (na - len(LA.act_tiles)) if L is LB else 0)
                    dve.wait_ge(s["g"], head * na + signs)
                    nc.vector.tensor_tensor(T[:, jt % NT, :], mask[:, jt, :], G[:, (k * na + n) % NG, :], ALU.is_gt)\
                        .then_inc(s["t"], 1)
                else:
                    nc.vector.scalar_tensor_tensor(
                        out=T[:, jt % NT, :], in0=F1N[:, k, :], scalar=L.S.t["nf2"][:, h, jt:jt + 1],
                        in1=mask[:, jt, :], op0=ALU.is_gt, op1=ALU.mult).then_inc(s["t"], 1)

        def dve_group(dve, b, par, L, g):
            s = L.S.s
            n = (EDGES[g + 1] - EDGES[g]) * P
            mask = mask_of(L, par)
            at = slice(EDGES[g] * P, EDGES[g + 1] * P)
            if g == 0:
                dve.wait_ge(s["f1_0"], L.turn(b) * 16 + 16)
                dve.wait_ge(s["c0"], 3 * L.turn(b) + 3)
                dve.wait_ge(s["xlo"], L.turn(b) * NTL + NTL)
            for jt in range(NTL):
                dve.wait_ge(s["t_used"], L.turn(b) * (NGR * NTL) + (g * NTL + jt + 1))
                nc.vector.scalar_tensor_tensor(
                    out=TW[:, jt, 0:n], in0=F1W[:, 0, at], scalar=L.S.t["nf2"][:, 0, jt:jt + 1],
                    in1=mask[:, jt, at], op0=ALU.is_gt, op1=ALU.mult).then_inc(s["t"], 1)

        def dve_combine_group(dve, b, L, g):
            s = L.S.s
            lo, hi = EDGES[g], EDGES[g + 1]
            n, bank = hi - lo, 4 + 2 * (g % 2)
            ut = uW[:, :].rearrange("p (t w) -> p t w", w=L.W)[:, lo:hi]
            tv, uv = (ps[:, bank + c, 0:n * L.W].rearrange("p (t w) -> p t w", w=L.W) for c in range(2))
            dve.wait_ge(s["t_used"], L.turn(b) * (NGR * NTL) + ((g + 1) * NTL + NTL))
            nc.vector.tensor_tensor(ut, uv, L.S.t["crow"][:, 0, lo:hi].unsqueeze(2).to_broadcast((P, n, L.W)),
                                    ALU.mult).then_inc(s["cmb"], 1)
            dve.wait_ge(s["cmb"], L.turn(b) * 6 + (g + 1))
            nc.vector.tensor_tensor(ut, ut, tv, ALU.add).then_inc(s["free"], 1)

        def dve_mean(dve, b, L):
            s, empty = L.S.s, L.S.t["empty"]
            dve.wait_ge(s["cmb"], L.turn(b) * 6 + 6 if L.wide else L.head(b, 0) * 6 + (6 * L.H + 1))
            dve.wait_ge(s["mean"], L.turn(b) + 1)
            mvw = L.S.t["meanb"][:, 0:L.H * L.W].rearrange("p (h w) -> p h w", w=L.W)[:, :, 0:L.D]
            for t in range(NTL):
                nc.vector.scalar_tensor_tensor(out=o_view(L)[:, t], in0=mvw, scalar=empty[:, t:t + 1],
                                               in1=o_view(L)[:, t], op0=ALU.mult, op1=ALU.add).then_inc(s["fin"], 1)
            dve.wait_ge(s["fin"], L.turn(b) * NTL + NTL)

        def dve_min(dve, b, L):
            s, n, o, hf = L.S.s, NTL * L.HD, L.S.t["o"], L.S.t["hf"]
            nc.vector.tensor_scalar(hf[:, 0:n], o[:, 0:n], 0.0, None, ALU.min).then_inc(s["emin"], 1)

        def dve_elu(dve, b, L):
            s, n, o, hf = L.S.s, NTL * L.HD, L.S.t["o"], L.S.t["hf"]
            dve.wait_ge(s["eexp"], elu_turn(L, b) + 1)
            nc.vector.scalar_tensor_tensor(out=o[:, 0:n], in0=o[:, 0:n], scalar=0.0, in1=hf[:, 0:n],
                                           op0=ALU.max, op1=ALU.add).then_inc(s["elu"], 1)
            dve.wait_ge(s["elu"], elu_turn(L, b) + 1)

        @block.vector
        def _(dve):
            for s, n in ((SN.s["t"], 2 * NTL), (SN.s["t_used"], NT), (SN.s["free"], 2), (SN.s["cmb"], 1),
                         (SW.s["t"], NGR * NTL), (SW.s["u"], U0), (SW.s["t_used"], NTL), (SW.s["free"], 2),
                         (q["mask_out"], 16), (q["y1_out"], 16), (q["y2_out"], 16), (q["x1_out"], 16), (q["y2s"], 4),
                         (q["xsum"], 1), (q["x3"], 2), (q["out"], 16), (q["out_x"], 1), (q["y1s"], 2), (q["y1_in"], 16)):
                dve.sem_inc(s, n)
            wr = [0, 0]
            dve.wait_ge(q["w_in"], 17 * 16)

            def fold(dst, w, vec, H, D):
                av = atmp[:, 0:H * D].rearrange("p (h d) -> p h d", h=H)
                nc.vector.tensor_tensor(av, w, vec, ALU.mult).then_inc(q["wprod"], 1)
                wr[0] += 1
                dve.wait_ge(q["wprod"], wr[0])
                nc.vector.tensor_reduce(dst, av, axis=AX.X, op=ALU.add).then_inc(q["wred"], 1)
                wr[1] += 1
                dve.wait_ge(q["wred"], wr[1])

            for L in LAYERS:
                if L is LB:
                    av = abc[L].rearrange("p (h c d) -> p h c d", c=2, d=L.D)
                    vec = [av[:, :, c, :] for c in range(2)]
                else:
                    av = abc[L].rearrange("p (a c d) -> p a c d", a=1, c=2)
                    vec = [av[:, :, c, :].to_broadcast((P, L.H, L.D)) for c in range(2)]
                for c in range(2):
                    at = slice(L.HD + c * L.H, L.HD + (c + 1) * L.H)
                    for kk in range(L.K):
                        fold(wcat[L][:, kk, at], wcat[L][:, kk, 0:L.HD].rearrange("p (h d) -> p h d", h=L.H),
                             vec[c], L.H, L.D)
                    if L is LA:
                        fold(bcat[:, at], bcat[:, 0:L.HD].rearrange("p (h d) -> p h d", h=L.H), vec[c], L.H, L.D)
            dve.wait_ge(q["cst"], 9)

            def batchnorm(n):
                dve.wait_ge(q[f"y{n + 1}s"], B * HALVES + (2, 4)[n])
                nc.vector.bn_aggr(bmv[:, n, :], bst[n][:, :, :].rearrange("p a s -> p (a s)")).then_inc(q[f"bag{n}"], 1)
                dve.wait_ge(q[f"bag{n}"], 1)
                nc.vector.tensor_scalar(bsc[:, n, 0:1], bmv[:, n, 1:2], BN_EPS, None, ALU.add).then_inc(q[f"bag{n}"], 1)
                dve.wait_ge(q[f"bpow{n}"], 1)
                nc.vector.tensor_tensor(bsc[:, n, 2:3], bsc[:, n, 1:2], cols[:, 3 * n + 1:3 * n + 2], ALU.mult)\
                    .then_inc(q[f"bs{n}"], 1)
                dve.wait_ge(q[f"bs{n}"], 1)
                nc.vector.tensor_tensor(bsc[:, n, 1:2], bsc[:, n, 2:3], bmv[:, n, 0:1], ALU.mult)\
                    .then_inc(q[f"bs{n}"], 1)
                dve.wait_ge(q[f"bs{n}"], 2)
                nc.vector.tensor_tensor(bsc[:, n, 3:4], cols[:, 3 * n + 2:3 * n + 3], bsc[:, n, 1:2], ALU.subtract)\
                    .then_inc(q[f"bt{n}"], 1)

            def n_piece(name, b, par, L):
                if name == "nB":
                    dve_b(dve, b, L)
                elif name == "nC":
                    dve_c(dve, b, L)
                elif name == "nm":
                    dve_m(dve, b, L)
                elif name == "nD":
                    dve_d(dve, b, L)
                elif name == "nE":
                    dve_e(dve, b, L)
                elif name[0] == "S":
                    dve_thresholds(dve, b, par, L, int(name[1]))
                elif name[0] == "K":
                    dve_combine(dve, b, L, int(name[1]))

            flat = "p (t f) -> p t f"

            def piece_a(name, b, par):
                n_piece(name, b, par, LA)
                if name == "nA":
                    dve.wait_ge(q["x_in"], b * 16 + 16)
                    dve_norm(dve, SN, norm_turn(LA, b), x_of(par))
                elif name == "nC":
                    dve.wait_ge(q["mT"], b * NTL + NTL)
                    nc.vector.tensor_scalar(SN.t["empty"][:, :], outdeg[:, :], 0.0, None, ALU.is_equal)\
                        .then_inc(q["deg0"], 1)
                    nc.vector.tensor_scalar(rin[:, :], indeg[:, :], 1.0, None, ALU.max).then_inc(q["deg0"], 1)
                    dve.wait_ge(q["deg0"], 2 * b + 2)
                    nc.vector.tensor_copy(empty_all[:, b, :], SN.t["empty"][:, :]).then_inc(q["deg"], 1)
                    nc.vector.reciprocal(rin_all[:, b, :], rin[:, :]).then_inc(q["deg"], 1)
                elif name == "nF":
                    dve_mean(dve, b, LA)
                    dve.wait_ge(q["x1_out"], b * 16 + 16)
                    nc.vector.tensor_tensor(xcW[:, :, :], x_of(par)[:, :, :], oN[:, 0:N].rearrange(flat, f=F), ALU.add)\
                        .then_inc(q["x1"], 1)
                elif name == "PA":
                    dve.wait_ge(q["x1"], b + 1)
                    dve_stats(dve, SW, norm_turn(None, b), xcW)
                elif name == "PB":
                    r1 = oW[:, :].rearrange(flat, f=F)
                    dve.wait_ge(q["hi"], b + 1)
                    nc.vector.scalar_tensor_tensor(out=r1, in0=xnW[:, :, :], scalar=0.0, in1=parts[1][:, :, 0, :],
                                                   op0=ALU.max, op1=ALU.subtract).then_inc(q["r1"], 1)
                    dve.wait_ge(q["mid"], b + 1)
                    nc.vector.tensor_tensor(parts[1][:, :, 2, :], r1, parts[1][:, :, 1, :], ALU.subtract)\
                        .then_inc(q["lo"], 1)
                elif name == "PC":
                    for h in range(HALVES):
                        dve.wait_ge(q["y1"], 2 * b + (h + 1))
                        nc.vector.bn_stats(bst[0][:, b * HALVES + h, :], hfW[:, h * BANK:(h + 1) * BANK])\
                            .then_inc(q["y1s"], 1)

            def piece_b(name, b, par):
                if name == "Ba":
                    r1 = oN[:, 0:N].rearrange(flat, f=F)
                    dve.wait_ge(q["lo"], b + B)
                    dve.wait_ge(q["hi"], b + (B + 1))
                    nc.vector.tensor_tensor(r1, xnN[:, :, :], parts[par][:, :, 0, :], ALU.subtract)\
                        .then_inc(q["r1"], 1)
                    dve.wait_ge(q["mid"], b + (B + 1))
                    nc.vector.tensor_tensor(parts[par][:, :, 2, :], r1, parts[par][:, :, 1, :], ALU.subtract)\
                        .then_inc(q["lo"], 1)
                elif name == "Bg":
                    for h in range(HALVES):
                        dve.wait_ge(q["y2"], 2 * b + (h + 1))
                        nc.vector.bn_stats(bst[1][:, b * HALVES + h, :], hfW[:, h * BANK:(h + 1) * BANK])\
                            .then_inc(q["y2s"], 1)

            def piece_c(name, b, par):
                if name == "nA":
                    dve.wait_ge(q["x1_in"], b * 16 + 16)
                    dve.wait_ge(q["ynT_ps"], 2 * b + 2)
                    for h in range(HALVES):
                        xv = xcN[:, 4 * h:4 * h + 4, :]
                        nc.vector.tensor_tensor(xv, xv, ps[:, 2 + h, :].rearrange(flat, f=F), ALU.add)\
                            .then_inc(q["x2"], 1)
                    dve.wait_ge(q["x2"], 2 * b + 2)
                    dve_stats(dve, SN, norm_turn(LB, b), xcN)
                if name == "K0":
                    dve.wait_ge(q["emp"], b + 1)
                elif name == "S0":
                    dve.wait_ge(q["mask_in"], b * 16 + (16 * B + 16))
                n_piece(name, b, par, LB)
                if name == "nC":
                    nc.vector.tensor_copy(SN.t["empty"][:, :], empty_all[:, b, :]).then_inc(q["emp"], 1)
                elif name == "nF":
                    dve_mean(dve, b, LB)
                    dve_min(dve, b, LB)
                elif name == "nG":
                    dve_elu(dve, b, LB)
                elif name in ("CB", "DB"):
                    dve_b(dve, b, wide_of(name))
                elif name in ("CC", "DC"):
                    dve_c(dve, b, wide_of(name))
                elif name in ("Cm", "Dm"):
                    dve_m(dve, b, wide_of(name))
                elif name in ("CD", "DD"):
                    dve_d(dve, b, wide_of(name))
                elif name == "DE":
                    dve_e(dve, b, LD)
                elif name == "CA":
                    nc.vector.tensor_copy(SW.t["empty"][:, :], empty_all[:, b, :]).then_inc(q["empW"], 1)
                elif name == "DA":
                    dve_stats(dve, SW, norm_turn(LD, b), xcW)
                elif name in ("c0", "c1", "c2", "d0", "d1", "d2"):
                    L, g = wide_of(name), int(name[1])
                    dve_group(dve, b, par, L, g)
                    if g:
                        dve_combine_group(dve, b, L, g - 1)
                if name in ("CF", "DF"):
                    L = wide_of(name)
                    dve.wait_ge(q["empW"], b + 1)
                    dve_combine_group(dve, b, L, NGR - 1)
                    dve.wait_ge(SW.s["free"], L.turn(b) * NGR + (NGR + 2))
                    dve_divide(dve, L, 0, uW[:, :].rearrange("p (t w) -> p t w", w=L.W), L.turn(b) * 6 + NGR)
                    dve_mean(dve, b, L)
                    dve_min(dve, b, L)
                    dve_elu(dve, b, L)
                    ov = oW[:, :].rearrange(flat, f=F)
                    if L is LC:
                        dve.wait_ge(q["out"], b * 16 + 16)
                        nc.vector.scalar_tensor_tensor(out=xcW[:, :, :], in0=ov, scalar=-1.0, in1=xsN[:, :, :],
                                                       op0=ALU.add, op1=ALU.add).then_inc(q["out_x"], 1)
                        dve.wait_ge(q["out_x"], b + 2)
                    else:
                        nc.vector.scalar_tensor_tensor(out=xcW[:, :, :], in0=ov, scalar=-1.0, in1=xcW[:, :, :],
                                                       op0=ALU.add, op1=ALU.add).then_inc(q["x3"], 1)

            walk(dve, ORDER_A, piece_a)
            batchnorm(0)
            walk(dve, ORDER_B, piece_b)
            batchnorm(1)
            walk(dve, ORDER_C, piece_c)

        def free_banks(pe, b, L):
            pe.wait_ge(L.S.s["free"], (L.turn(b) * NGR if L.wide else L.head(b, 0)) + 2)

        def pe_b(pe, b, L):
            s, ff, xn = L.S.s, L.S.t["ff"], L.S.t["xn"]
            free_banks(pe, b, L)
            for k in range(L.K):
                for t in range(NTL):
                    if L is LC:
                        if k == 0 and t == 0:
                            pe.wait_ge(SN.s["elu"], b + 1)
                        src = oN[:, :].rearrange("p (t k f) -> p t k f", k=L.K, f=P)[:, t, k, :]
                    else:
                        pe.wait_ge(s["xn"], norm_turn(L, b) * NTL + (t + 1))
                        src = xn[:, t, :]
                    tr = nc.tensor.transpose(ps[:, hT_bank(L, k * HALVES + t // 4), (t % 4) * P:(t % 4 + 1) * P], src,
                                             identF[:, :])
                    if t % 4 == 3:
                        tr.then_inc(s["hT_ps"], 1)
            for t in range(NTL):
                pe.wait_ge(s["hinT"], hT_before(L, b) + (L.K * HALVES if L.K > 1 else t // 4 + 1))
                if t >= 2:
                    pe.wait_ge(s["hf"], L.turn(b) * (NTL + 1) + t)
                for k in range(L.K):
                    mm = nc.tensor.matmul(ps[:, proj_bank(L, t), 0:L.NC],
                                          hinT_of(L)[:, k * N + t * P:k * N + (t + 1) * P],
                                          wcat[L][:, k, :], start=(k == 0), stop=(k == L.K - 1))
                mm.then_inc(s["proj_ps"], 1)

        def pe_c(pe, b, L):
            s, ff, H2 = L.S.s, L.S.t["ff"], 2 * L.H
            fb, mb = (4, 6) if L.wide else (2, 0)
            for t in range(NTL):
                pe.wait_ge(s["f"], L.turn(b) * NTL + (t + 1))
                tr = nc.tensor.transpose(ps[0:H2, fb + t // 4, (t % 4) * P:(t % 4 + 1) * P], ff[:, 0:H2, t],
                                         identF[:, :])
                if t % 4 == 3:
                    tr.then_inc(s["frow_ps"], 1)
            pe.wait_ge(s["hf"], L.turn(b) * (NTL + 1) + (NTL + 1))
            for t in range(NTL):
                mm = nc.tensor.matmul(ps[:, mb, 0:L.H * L.W], cmean[:, :],
                                      L.S.t["hf"][:, t * L.H * L.W:(t + 1) * L.H * L.W], start=(t == 0),
                                      stop=(t == NTL - 1))
            mm.then_inc(s["mean_ps"], 1)

        def pe_m(pe, b, L):
            s, H2, mb = L.S.s, 2 * L.H, 6 if L.wide else 0
            pe.wait_ge(s["diag"], L.turn(b) + 1)
            nc.tensor.matmul(ps[:, mb + 1, 0:H2], ones[0:H2, :], L.S.t["diag"][0:H2, 0:H2], start=True, stop=True)\
                .then_inc(s["m2_ps"], 1)

        def pe_sums(pe, b, par, L, tiles):
            s, xv, mask = L.S.s, xp_view(L), mask_of(L, par)
            pe.wait_ge(s["mean"], L.turn(b) + 1)
            pe.wait_ge(s["m2"], L.turn(b) + 1)
            for it in tiles:
                if it >= 4:
                    pe.wait_ge(s["ms"], L.turn(b) * NTL + (it - 3 if it < 6 else it - 1))
                for jt in range(NTL):
                    if it == 0:
                        pe.wait_ge(s["xlo"], L.turn(b) * NTL + (jt + 1))
                    for part in range(3):
                        mm = nc.tensor.matmul(ps[:, ms_bank(it), 0:L.H * L.W], mask[:, jt, it * P:(it + 1) * P],
                                              xv[:, jt, part, :, 1, :], start=(jt == 0 and part == 0),
                                              stop=(jt == NTL - 1 and part == 2))
                mm.then_inc(s["ms_ps"], 1)

        def pe_head(pe, b, L, h):
            s, xv, k = L.S.s, xp_view(L), 1 - h % 2
            head = L.head(b, h)
            pe.wait_ge(s["free"], head + 1)
            if h < 2:
                pe.wait_ge(s["ms"], L.turn(b) * NTL + (NTL if h else 4))
            for jt in range(NTL):
                pe.wait_ge(s["t"], head * NTL + (2 * NTL + jt + 1))
                for it in range(NTL):
                    for part in range(3):
                        mm = nc.tensor.matmul(
                            ps[:, 2 * k + it // 4, (it % 4) * 2 * L.W:(it % 4 + 1) * 2 * L.W],
                            T[:, jt % NT, it * P:(it + 1) * P], xv[:, jt, part, h],
                            start=(jt == 0 and it % 4 == 0 and part == 0),
                            stop=(jt == NTL - 1 and it % 4 == 3 and part == 2), skip_group_check=True)
                mm.then_inc(s["t_used"], 1)

        def pe_group(pe, b, L, g):
            s, xv, bank = L.S.s, xp_view(L), 4 + 2 * (g % 2)
            pe.wait_ge(s["free"], L.turn(b) * NGR + (g + 1))
            if g == 0:
                pe.wait_ge(s["xlo"], L.turn(b) * NTL + NTL)
            if g == 1:
                pe.wait_ge(s["mean"], L.turn(b) + 1)
                pe.wait_ge(s["m2"], L.turn(b) + 1)
            for jt in range(NTL):
                at = L.turn(b) * (NGR * NTL) + (g * NTL + jt + 1)
                for c, tile in enumerate((TW, UW)):
                    pe.wait_ge(s["tu"[c]], at + (U0 if c else NGR * NTL))
                    for n in range(EDGES[g + 1] - EDGES[g]):
                        for part in range(3):
                            mm = nc.tensor.matmul(
                                ps[:, bank + c, n * L.W:(n + 1) * L.W], tile[:, jt, n * P:(n + 1) * P],
                                xv[:, jt, part, 0, c, :], start=(jt == 0 and n == 0 and part == 0),
                                stop=(jt == NTL - 1 and n == EDGES[g + 1] - EDGES[g] - 1 and part == 2),
                                skip_group_check=True)
                mm.then_inc(s["t_used"], 1)

        @block.tensor
        def _(pe):
            pe.wait_ge(q["cst"], 9)
            pe.wait_ge(q["wred"], 12)

            def n_piece(name, b, par, L):
                if name == "nB":
                    pe_b(pe, b, L)
                elif name == "nC":
                    pe_c(pe, b, L)
                elif name == "nm":
                    pe_m(pe, b, L)
                elif name in ("M0", "M1"):
                    pe_sums(pe, b, par, L, SUMS[name])
                elif name[0] == "T":
                    pe_head(pe, b, L, int(name[1]))

            def piece_a(name, b, par):
                n_piece(name, b, par, LA)
                if name == "XT":
                    pe.wait_ge(q["adj_cvt"], b * NTL + (NTL + NS))
                    for t in range(NTL):
                        if t >= 4:
                            pe.wait_ge(q["mT"], b * NTL + (t - 3))
                        for it in range(NTL):
                            tr = nc.tensor.transpose(ps[:, 4 + t % 4, :].bitcast(BF16)[:, it * P:(it + 1) * P],
                                                     adj_nat[par][:, it, t * P:(t + 1) * P], identB[:, :])
                        tr.then_inc(q["mT_ps"], 1)
                elif name == "Pz":
                    pe.wait_ge(q["y1"], 2 * b + 2)
                elif name == "Xz":
                    pe.wait_ge(q["mT"], b * NTL + NTL)
                elif name == "PG":
                    pe.wait_ge(q["lo"], b + 1)
                    for rt in range(NTL):
                        if rt >= 4:
                            pe.wait_ge(q["reg"], b * NTL + (rt - 3))
                        for t in range(NTL):
                            for part in range(3):
                                mm = nc.tensor.matmul(ps[:, 4 + rt % 4, 0:P], adj_nat[par][:, t, rt * P:(rt + 1) * P],
                                                      parts[1][:, t, part, :],
                                                      start=(t == 0 and part == 0), stop=(t == NTL - 1 and part == 2))
                        mm.then_inc(q["reg_ps"], 1)
                elif name == "PC":
                    pe.wait_ge(q["reg"], b * NTL + NTL)
                    for t in range(NTL):
                        tr = nc.tensor.transpose(ps[:, 4 + t // 4, (t % 4) * P:(t % 4 + 1) * P], xnW[:, t, :],
                                                 identF[:, :])
                        if t % 4 == 3:
                            tr.then_inc(q["regT_ps"], 1)
                    for h in range(HALVES):
                        pe.wait_ge(q["regT"], 2 * b + (h + 1))
                        nc.tensor.matmul(ps[:, 6 + h, :], k1s[:, :], oW[:, h * BANK:(h + 1) * BANK],
                                         start=True, stop=True).then_inc(q["y1_ps"], 1)

            def piece_b(name, b, par):
                if name == "Ba":
                    pe.wait_ge(q["z"], b + 3)
                    for t in range(NTL):
                        mm = nc.tensor.matmul(ps[:, 4 + t // 4, (t % 4) * P:(t % 4 + 1) * P],
                                              scratch[:, t * P:(t + 1) * P], k2s[:, :], start=True, stop=True)
                        if t % 4 == 3:
                            mm.then_inc(q["G_ps"], 1)
                elif name == "Bg":
                    pe.wait_ge(q["lo"], b + (B + 1))
                    pe.wait_ge(q["mask_in"], b * 16 + 16)
                    for h in range(HALVES):
                        for t in range(NTL):
                            for part in range(3):
                                mm = nc.tensor.matmul(ps[:, 2 * par + h, :], parts[par][:, t, part, :],
                                                      maskbuf[:, par, t, h * BANK:(h + 1) * BANK],
                                                      start=(t == 0 and part == 0), stop=(t == NTL - 1 and part == 2))
                        mm.then_inc(q["y2_ps"], 1)

            def piece_c(name, b, par):
                if name == "ny":
                    pe.wait_ge(q["yn"], b + 1)
                    pe.wait_ge(SN.s["free"], LB.head(b, 0) + 1)
                    for t in range(NTL):
                        tr = nc.tensor.transpose(ps[:, 2 + t // 4, (t % 4) * P:(t % 4 + 1) * P],
                                                 xnN[:, t, :], identF[:, :])
                        if t % 4 == 3:
                            tr.then_inc(q["ynT_ps"], 1)
                if name == "M0":
                    pe.wait_ge(q["mask_in"], b * 16 + (16 * B + 16))
                n_piece(name, b, par, LB)
                if name in ("CB", "DB"):
                    pe_b(pe, b, wide_of(name))
                elif name in ("CC", "DC"):
                    pe_c(pe, b, wide_of(name))
                elif name in ("Cm", "Dm"):
                    pe_m(pe, b, wide_of(name))
                elif name in ("C0", "C1", "C2", "D0", "D1", "D2"):
                    pe_group(pe, b, wide_of(name), int(name[1]))

            walk(pe, ORDER_A, piece_a)
            walk(pe, ORDER_B, piece_b)
            walk(pe, ORDER_C, piece_c)


_INS = ['x', 'adj', 'L0_gnn_W', 'L0_gnn_b', 'L0_gnn_a', 'L1_gnn_kernel_1', 'L1_gnn_bias_1', 'L1_gnn_gamma_1',
        'L1_gnn_beta_1', 'L1_gnn_kernel_2', 'L1_gnn_bias_2', 'L1_gnn_gamma_2', 'L1_gnn_beta_2', 'L2_gnn_W1',
        'L2_gnn_a1', 'L2_gnn_W2', 'L2_gnn_a2', 'L3_gnn_W', 'L3_gnn_a']


def kernel(**inputs):
    import numpy as _np
    import concourse.bacc as _bacc
    from concourse import mybir as _mybir
    from concourse.bass_utils import run_bass_kernel_spmd as _run

    nc = _bacc.Bacc("TRN2", target_bir_lowering=False, num_devices=1)
    arrays, args = {}, []
    for name in _INS:
        a = _np.ascontiguousarray(inputs[name])
        arrays[f"in_{name}"] = a
        args.append(nc.dram_tensor(f"in_{name}", a.shape, _mybir.dt.from_np(a.dtype), kind="ExternalInput").ap())
    x = inputs["x"]
    o = nc.dram_tensor("out", tuple(x.shape), _mybir.dt.float32, kind="ExternalOutput").ap()
    gnn_stack(nc, *args, o)
    r = _run(nc, [arrays], core_ids=[0])
    return r.results[0]["out"]
```
